# Optimizing a Trainium2 kernel written in Bass

```python
import numpy as np
import jax
import jax.numpy as jnp

def _softmax(x, axis=-1):
    return jax.nn.softmax(x, axis=axis)

def _gelu(x):
    return jax.nn.gelu(x, approximate=True)

def _silu(x):
    return jax.nn.silu(x)

def _sigmoid(x):
    return jax.nn.sigmoid(x)

def _layernorm(x, axis=-1, eps=1e-05):
    m = jnp.mean(x, axis=axis, keepdims=True)
    v = jnp.var(x, axis=axis, keepdims=True)
    return (x - m) / jnp.sqrt(v + eps)

def _scatter_add(tgt, idx, src, axis=0):
    return tgt.at[idx].add(src)

def _segment_sum(src, seg, n):
    return jax.ops.segment_sum(src, seg, n)
kernel_name = 'mk_audio_tower_d1_tok_audfeat1024_r4_b6c59b'

def setup_inputs(seed: int=0):
    np.random.seed(seed)
    _w = jnp.asarray

    def _rec_inputs():
        import jax
        import jax.numpy as jnp
        _rk = jax.random.key(seed)
        x = 0.00021031 + 1.00007 * jax.random.normal(jax.random.fold_in(_rk, 1), (8, 750, 256), jnp.float32)
        return x
    x = _rec_inputs()

    def _L0_tok_setup():
        import jax, jax.numpy as jnp
        import numpy as np
        DIM = 256
        SEGMENT_SIZE = 256
        DILATION_RATE = 2
        key = jax.random.key(seed)
        x = jax.random.normal(key, (4, 2048, DIM), dtype=jnp.float32)
        return {'x': x}
    _L0_tok_all = _L0_tok_setup()
    _L0_tok_in = {k: v for k, v in _L0_tok_all.items() if k in ()}
    del _L0_tok_all

    def _L0_attn_setup():
        import jax, jax.numpy as jnp
        import numpy as np
        DIM = 256

        def _circ_conv(x, key):
            D = x.shape[-1]
            return jnp.fft.irfft(jnp.fft.rfft(x, axis=-1) * jnp.fft.rfft(key), n=D, axis=-1)

        def _circ_corr(x, key):
            D = x.shape[-1]
            return jnp.fft.irfft(jnp.fft.rfft(x, axis=-1) * jnp.conj(jnp.fft.rfft(key)), n=D, axis=-1)
        key = jax.random.key(seed)
        k0, k1, k2 = jax.random.split(key, 3)
        B, T, D = (4, 512, DIM)
        x = jax.random.normal(k0, (B, T, D), dtype=jnp.float32)
        bind_key = jax.random.normal(k1, (D,), dtype=jnp.float32) * 0.02
        unbind_key = jax.random.normal(k2, (D,), dtype=jnp.float32) * 0.02
        gate = jnp.ones((1,), dtype=jnp.float32)
        decay = jnp.asarray(0.9, dtype=jnp.float32)
        return {'x': x, 'bind_key': bind_key, 'unbind_key': unbind_key, 'gate': gate, 'decay': decay}
    _L0_attn_all = _L0_attn_setup()
    _L0_attn_in = {k: v for k, v in _L0_attn_all.items() if k in ('bind_key', 'unbind_key', 'gate', 'decay')}
    del _L0_attn_all

    def _L0_ffn_setup():
        import jax, jax.numpy as jnp
        import numpy as np
        B, N, D = (4, 1024, 256)
        E, K, H, ITERS = (8, 2, 64, 2)
        DT = 0.1
        C = 2 * D

        def _gelu(x):
            return jax.nn.gelu(x, approximate=False)

        def _inl(ctrl, xs, vs, mu):
            a, b, g = jnp.split(ctrl, 3, axis=-1)
            v_next = jax.nn.sigmoid(a) * vs - jax.nn.softplus(b) * (xs - mu)
            x_next = xs + DT * jax.nn.sigmoid(g) * v_next
            return (x_next, v_next)

        def _experts(ctx, idx, w1, b1, w2, b2):
            out = jnp.zeros((ctx.shape[0], w2.shape[2]), ctx.dtype)
            for e in range(E):
                h = _gelu(ctx @ w1[e] + b1[e])
                o = h @ w2[e] + b2[e]
                out = out + jnp.where((idx == e)[:, None], o, jnp.float32(0))
            return out

        def _forward(x, integration_weight, mu, router_w1, router_b1, router_w2, router_b2, halt_w1, halt_b1, halt_w2, halt_b2, expert_w1, expert_b1, expert_w2, expert_b2, shared_w1, shared_b1, shared_w2, shared_b2, shared_weight, refine_w1, refine_b1, refine_w2, refine_b2):
            b, n, d = x.shape
            xf = x.reshape(b * n, d)
            logits = _gelu(xf @ router_w1 + router_b1) @ router_w2 + router_b2
            probs = jax.nn.softmax(logits, axis=-1)
            topk_p, topk_i = jax.lax.top_k(probs, K)
            topk_p = topk_p / jnp.sum(topk_p, axis=-1, keepdims=True)
            flat_idx = topk_i.reshape(-1)
            flat_w = topk_p.reshape(-1, 1)
            v = jnp.zeros_like(xf)
            integrated = xf
            for _ in range(ITERS):
                ctx = jnp.concatenate([integrated, v], axis=-1)
                shared_ctrl = _gelu(ctx @ shared_w1 + shared_b1) @ shared_w2 + shared_b2
                x_sh, v_sh = _inl(shared_ctrl, integrated, v, mu)
                sw = jax.nn.sigmoid(shared_weight)
                ctx_e = jnp.repeat(ctx, K, axis=0)
                x_e = jnp.repeat(integrated, K, axis=0)
                v_e = jnp.repeat(v, K, axis=0)
                ctrl = _experts(ctx_e, flat_idx, expert_w1, expert_b1, expert_w2, expert_b2)
                x_r, v_r = _inl(ctrl, x_e, v_e, mu)
                x_r = (x_r * flat_w).reshape(-1, K, d).sum(axis=1)
                v_r = (v_r * flat_w).reshape(-1, K, d).sum(axis=1)
                x_next = sw * x_sh + (1.0 - sw) * x_r
                v_next = sw * v_sh + (1.0 - sw) * v_r
                halt = jax.nn.sigmoid(_gelu(integrated @ halt_w1 + halt_b1) @ halt_w2 + halt_b2)
                integrated = integrated + halt * (x_next - integrated)
                v = v + halt * (v_next - v)
            refined = _gelu(integrated @ refine_w1 + refine_b1) @ refine_w2 + refine_b2
            out = xf + integration_weight * refined
            return out.reshape(b, n, d)
        key = jax.random.key(seed)
        ks = jax.random.split(key, 12)
        rn = lambda k, s, sc=0.02: jax.random.normal(k, s, dtype=jnp.float32) * sc
        z = lambda s: jnp.zeros(s, jnp.float32)
        return {'x': jax.random.normal(ks[0], (B, N, D), dtype=jnp.float32), 'integration_weight': jnp.full((D,), 0.5, jnp.float32), 'mu': z((D,)), 'router_w1': rn(ks[1], (D, D // 4)), 'router_b1': z((D // 4,)), 'router_w2': rn(ks[2], (D // 4, E)), 'router_b2': z((E,)), 'halt_w1': rn(ks[3], (D, D // 4)), 'halt_b1': z((D // 4,)), 'halt_w2': rn(ks[4], (D // 4, 1)), 'halt_b2': z((1,)), 'expert_w1': rn(ks[5], (E, C, H)), 'expert_b1': z((E, H)), 'expert_w2': rn(ks[6], (E, H, 3 * D)), 'expert_b2': z((E, 3 * D)), 'shared_w1': rn(ks[7], (C, H)), 'shared_b1': z((H,)), 'shared_w2': rn(ks[8], (H, 3 * D)), 'shared_b2': z((3 * D,)), 'shared_weight': jnp.float32(0.5), 'refine_w1': rn(ks[9], (D, 2 * D)), 'refine_b1': z((2 * D,)), 'refine_w2': rn(ks[10], (2 * D, D)), 'refine_b2': z((D,))}
    _L0_ffn_all = _L0_ffn_setup()
    _L0_ffn_in = {k: v for k, v in _L0_ffn_all.items() if k in ('integration_weight', 'mu', 'router_w1', 'router_b1', 'router_w2', 'router_b2', 'halt_w1', 'halt_b1', 'halt_w2', 'halt_b2', 'expert_w1', 'expert_b1', 'expert_w2', 'expert_b2', 'shared_w1', 'shared_b1', 'shared_w2', 'shared_b2', 'shared_weight', 'refine_w1', 'refine_b1', 'refine_w2', 'refine_b2')}
    del _L0_ffn_all
    return {'x': x, 'L0_attn_bind_key': _L0_attn_in['bind_key'], 'L0_attn_unbind_key': _L0_attn_in['unbind_key'], 'L0_attn_gate': _L0_attn_in['gate'], 'L0_attn_decay': _L0_attn_in['decay'], 'L0_ffn_integration_weight': _L0_ffn_in['integration_weight'], 'L0_ffn_mu': _L0_ffn_in['mu'], 'L0_ffn_router_w1': _L0_ffn_in['router_w1'], 'L0_ffn_router_b1': _L0_ffn_in['router_b1'], 'L0_ffn_router_w2': _L0_ffn_in['router_w2'], 'L0_ffn_router_b2': _L0_ffn_in['router_b2'], 'L0_ffn_halt_w1': _L0_ffn_in['halt_w1'], 'L0_ffn_halt_b1': _L0_ffn_in['halt_b1'], 'L0_ffn_halt_w2': _L0_ffn_in['halt_w2'], 'L0_ffn_halt_b2': _L0_ffn_in['halt_b2'], 'L0_ffn_expert_w1': _L0_ffn_in['expert_w1'], 'L0_ffn_expert_b1': _L0_ffn_in['expert_b1'], 'L0_ffn_expert_w2': _L0_ffn_in['expert_w2'], 'L0_ffn_expert_b2': _L0_ffn_in['expert_b2'], 'L0_ffn_shared_w1': _L0_ffn_in['shared_w1'], 'L0_ffn_shared_b1': _L0_ffn_in['shared_b1'], 'L0_ffn_shared_w2': _L0_ffn_in['shared_w2'], 'L0_ffn_shared_b2': _L0_ffn_in['shared_b2'], 'L0_ffn_shared_weight': _L0_ffn_in['shared_weight'], 'L0_ffn_refine_w1': _L0_ffn_in['refine_w1'], 'L0_ffn_refine_b1': _L0_ffn_in['refine_b1'], 'L0_ffn_refine_w2': _L0_ffn_in['refine_w2'], 'L0_ffn_refine_b2': _L0_ffn_in['refine_b2']}

def reference(x, L0_attn_bind_key, L0_attn_unbind_key, L0_attn_gate, L0_attn_decay, L0_ffn_integration_weight, L0_ffn_mu, L0_ffn_router_w1, L0_ffn_router_b1, L0_ffn_router_w2, L0_ffn_router_b2, L0_ffn_halt_w1, L0_ffn_halt_b1, L0_ffn_halt_w2, L0_ffn_halt_b2, L0_ffn_expert_w1, L0_ffn_expert_b1, L0_ffn_expert_w2, L0_ffn_expert_b2, L0_ffn_shared_w1, L0_ffn_shared_b1, L0_ffn_shared_w2, L0_ffn_shared_b2, L0_ffn_shared_weight, L0_ffn_refine_w1, L0_ffn_refine_b1, L0_ffn_refine_w2, L0_ffn_refine_b2):
    import jax
    import jax.numpy as jnp

    def _L0_tok_ref(x):
        import jax, jax.numpy as jnp
        import numpy as np
        DIM = 256
        SEGMENT_SIZE = 256
        DILATION_RATE = 2
        B, S, D = x.shape
        pad = -S % SEGMENT_SIZE
        x = jnp.pad(x, ((0, 0), (0, pad), (0, 0)))
        x = x.reshape(B, -1, SEGMENT_SIZE, D)
        x = x[:, :, ::DILATION_RATE, :]
        q = k = v = x
        scale = 1.0 / jnp.sqrt(jnp.asarray(D, dtype=x.dtype))
        scores = jnp.einsum('bsqd,bskd->bsqk', q, k) * scale
        probs = jax.nn.softmax(scores, axis=-1)
        attn = jnp.einsum('bsqk,bskd->bsqd', probs, v)
        return attn.reshape(B, -1, D)

    def _L0_attn_ref(x, bind_key, unbind_key, gate, decay):
        import jax, jax.numpy as jnp
        import numpy as np
        DIM = 256

        def _circ_conv(x, key):
            D = x.shape[-1]
            return jnp.fft.irfft(jnp.fft.rfft(x, axis=-1) * jnp.fft.rfft(key), n=D, axis=-1)

        def _circ_corr(x, key):
            D = x.shape[-1]
            return jnp.fft.irfft(jnp.fft.rfft(x, axis=-1) * jnp.conj(jnp.fft.rfft(key)), n=D, axis=-1)
        B, T, D = x.shape
        bound = _circ_conv(x, bind_key)
        d = jax.nn.sigmoid(decay)
        pos = jnp.arange(T, dtype=x.dtype)
        diff = pos[:, None] - pos[None, :]
        causal = diff >= 0
        decay_matrix = jnp.where(causal, d ** jnp.maximum(diff, 0.0), 0.0)
        hologram = jnp.einsum('ts,bsd->btd', decay_matrix, bound)
        retrieved = _circ_corr(hologram, unbind_key)
        return x + gate * retrieved

    def _L0_ffn_ref(x, integration_weight, mu, router_w1, router_b1, router_w2, router_b2, halt_w1, halt_b1, halt_w2, halt_b2, expert_w1, expert_b1, expert_w2, expert_b2, shared_w1, shared_b1, shared_w2, shared_b2, shared_weight, refine_w1, refine_b1, refine_w2, refine_b2):
        import jax, jax.numpy as jnp
        import numpy as np
        B, N, D = (4, 1024, 256)
        E, K, H, ITERS = (8, 2, 64, 2)
        DT = 0.1
        C = 2 * D

        def _gelu(x):
            return jax.nn.gelu(x, approximate=False)

        def _inl(ctrl, xs, vs, mu):
            a, b, g = jnp.split(ctrl, 3, axis=-1)
            v_next = jax.nn.sigmoid(a) * vs - jax.nn.softplus(b) * (xs - mu)
            x_next = xs + DT * jax.nn.sigmoid(g) * v_next
            return (x_next, v_next)

        def _experts(ctx, idx, w1, b1, w2, b2):
            out = jnp.zeros((ctx.shape[0], w2.shape[2]), ctx.dtype)
            for e in range(E):
                h = _gelu(ctx @ w1[e] + b1[e])
                o = h @ w2[e] + b2[e]
                out = out + jnp.where((idx == e)[:, None], o, jnp.float32(0))
            return out

        def _forward(x, integration_weight, mu, router_w1, router_b1, router_w2, router_b2, halt_w1, halt_b1, halt_w2, halt_b2, expert_w1, expert_b1, expert_w2, expert_b2, shared_w1, shared_b1, shared_w2, shared_b2, shared_weight, refine_w1, refine_b1, refine_w2, refine_b2):
            b, n, d = x.shape
            xf = x.reshape(b * n, d)
            logits = _gelu(xf @ router_w1 + router_b1) @ router_w2 + router_b2
            probs = jax.nn.softmax(logits, axis=-1)
            topk_p, topk_i = jax.lax.top_k(probs, K)
            topk_p = topk_p / jnp.sum(topk_p, axis=-1, keepdims=True)
            flat_idx = topk_i.reshape(-1)
            flat_w = topk_p.reshape(-1, 1)
            v = jnp.zeros_like(xf)
            integrated = xf
            for _ in range(ITERS):
                ctx = jnp.concatenate([integrated, v], axis=-1)
                shared_ctrl = _gelu(ctx @ shared_w1 + shared_b1) @ shared_w2 + shared_b2
                x_sh, v_sh = _inl(shared_ctrl, integrated, v, mu)
                sw = jax.nn.sigmoid(shared_weight)
                ctx_e = jnp.repeat(ctx, K, axis=0)
                x_e = jnp.repeat(integrated, K, axis=0)
                v_e = jnp.repeat(v, K, axis=0)
                ctrl = _experts(ctx_e, flat_idx, expert_w1, expert_b1, expert_w2, expert_b2)
                x_r, v_r = _inl(ctrl, x_e, v_e, mu)
                x_r = (x_r * flat_w).reshape(-1, K, d).sum(axis=1)
                v_r = (v_r * flat_w).reshape(-1, K, d).sum(axis=1)
                x_next = sw * x_sh + (1.0 - sw) * x_r
                v_next = sw * v_sh + (1.0 - sw) * v_r
                halt = jax.nn.sigmoid(_gelu(integrated @ halt_w1 + halt_b1) @ halt_w2 + halt_b2)
                integrated = integrated + halt * (x_next - integrated)
                v = v + halt * (v_next - v)
            refined = _gelu(integrated @ refine_w1 + refine_b1) @ refine_w2 + refine_b2
            out = xf + integration_weight * refined
            return out.reshape(b, n, d)
        return _forward(x, integration_weight, mu, router_w1, router_b1, router_w2, router_b2, halt_w1, halt_b1, halt_w2, halt_b2, expert_w1, expert_b1, expert_w2, expert_b2, shared_w1, shared_b1, shared_w2, shared_b2, shared_weight, refine_w1, refine_b1, refine_w2, refine_b2)
    h = _L0_tok_ref(x)
    h = h + _L0_attn_ref(_layernorm(h, axis=-1), L0_attn_bind_key, L0_attn_unbind_key, L0_attn_gate, L0_attn_decay)
    h = h + _L0_ffn_ref(_layernorm(h, axis=-1), L0_ffn_integration_weight, L0_ffn_mu, L0_ffn_router_w1, L0_ffn_router_b1, L0_ffn_router_w2, L0_ffn_router_b2, L0_ffn_halt_w1, L0_ffn_halt_b1, L0_ffn_halt_w2, L0_ffn_halt_b2, L0_ffn_expert_w1, L0_ffn_expert_b1, L0_ffn_expert_w2, L0_ffn_expert_b2, L0_ffn_shared_w1, L0_ffn_shared_b1, L0_ffn_shared_w2, L0_ffn_shared_b2, L0_ffn_shared_weight, L0_ffn_refine_w1, L0_ffn_refine_b1, L0_ffn_refine_w2, L0_ffn_refine_b2)
    return h

_drawn_inputs = setup_inputs


def setup_inputs(seed=0):
    import zlib

    import numpy as np

    out = dict(_drawn_inputs(seed))
    spreads = {'L0_ffn_integration_weight': (0.5, 0.6),
     'L0_ffn_mu': (0.0, 0.8),
     'L0_ffn_router_b1': (0.0, 2.0),
     'L0_ffn_router_b2': (0.0, 2.0),
     'L0_ffn_halt_b1': (0.0, 2.0),
     'L0_ffn_expert_b1': (0.0, 2.0),
     'L0_ffn_expert_b2': (0.0, 2.0),
     'L0_ffn_shared_b1': (0.0, 2.0),
     'L0_ffn_shared_b2': (0.0, 2.0),
     'L0_ffn_refine_b1': (0.0, 0.8),
     'L0_ffn_refine_b2': (0.0, 0.465)}
    factors = {'L0_ffn_router_w1': 35.096,
     'L0_ffn_router_w2': 25.572,
     'L0_ffn_halt_w1': 8.0,
     'L0_ffn_halt_w2': 8.0,
     'L0_ffn_expert_w1': 29.189,
     'L0_ffn_expert_w2': 25.077,
     'L0_ffn_shared_w1': 8.0,
     'L0_ffn_shared_w2': 8.0,
     'L0_ffn_refine_w1': 4.414,
     'L0_ffn_refine_w2': 4.101}
    for name, (base, spread) in spreads.items():
        noise = np.random.default_rng([zlib.crc32(name.encode()), seed]).standard_normal(out[name].shape)
        drawn = base * np.exp(spread * noise) if base else spread * noise
        out[name] = jnp.asarray(drawn.astype(out[name].dtype))
    for name, factor in factors.items():
        out[name] = (out[name] * factor).astype(out[name].dtype)
    return out
```

```python
import concourse.bass as bass
from concourse import mybir
from contextlib import ExitStack

P = 128
BATCH, SEQ, D = 8, 750, 256
SEG, DIL = 256, 2
NS = -(-SEQ // SEG)
NT = BATCH * NS
TAIL = (SEQ - (NS - 1) * SEG + DIL - 1) // DIL
E, HID, REF = 8, 64, 512
KD = D // P
EC = E * HID // P
BR = 3
LN_EPS = 1e-5

_FIRST = [("ident", P), ("expand", EC * P), ("iota", 3 * E), ("part", 3), ("shared_row", P),
          ("bind", KD * D), ("unbind", KD * D), ("decay", 1), ("gate", 1), ("sw", 1),
          ("w1r", KD * HID), ("b1r", 1), ("w2r", E), ("b2r", E), ("mu", D), ("iw", D), ("rb2", D)]
_SECOND = [("w1e", 2 * KD * E * HID), ("w1s", 2 * KD * P), ("w2e", EC * 3 * D), ("w2s", 3 * D), ("w2h", 1),
           ("r1", KD * REF), ("r2", REF // P * D), ("b2", 3 * D), ("b1e", EC), ("b1s", 1), ("rb1", REF // P),
           ("hb2", 1)]


def _offsets():
    at, out = 0, {}
    for name, n in _FIRST + _SECOND:
        out[name] = (at, n)
        at += n
    return out, at, sum(n for _, n in _FIRST)


OFF, NPARAM, NFIRST = _offsets()


class Tile:

    def __init__(self, b, s, low=None):
        self.b, self.s = b, s
        self.n = b * NS + s
        self.low = self.n if low is None else low

    def at(self, k):
        q, s = divmod(self.s + k, NS)
        return Tile(self.b + q, s, self.low + k)

    def exists(self):
        return not isinstance(self.n, int) or 0 <= self.n < NT


def passed(eng, sem, tile, back=0, per=1, plus=0):
    low = (tile.low - back + 1) * per + plus
    if isinstance(tile.n, int) and low <= 0:
        return
    assert low > 0
    eng.wait_ge(sem, (tile.n + (1 - back)) * per + plus)


DVE_LINKS = 28


def audio_layer(nc, x, params, out):
    fp32, bf16 = mybir.dt.float32, mybir.dt.bfloat16
    u32 = mybir.dt.uint32
    ALU, ACT, AX = mybir.AluOpType, mybir.ActivationFunctionType, mybir.AxisListType
    ctx = ExitStack()
    with ctx:
        def sb(name, shape, dt=fp32):
            return ctx.enter_context(nc.sbuf_tensor(name, shape, dt))

        def ps(name, cols):
            return ctx.enter_context(nc.psum_tensor(name, [P, cols], fp32))

        def sem(name):
            return ctx.enter_context(nc.semaphore(name))

        par = sb("par", [P, NPARAM])

        def pv(name, rows=P):
            a, n = OFF[name]
            return par[0:rows, a:a + n]

        ident = pv("ident")
        w1e = pv("w1e").rearrange("p (k c m) -> p k c m", k=2 * KD, c=EC)
        w1s = pv("w1s").rearrange("p (k m) -> p k m", k=2 * KD)
        w1r = pv("w1r").rearrange("p (k m) -> p k m", k=KD)
        w2e = pv("w2e").rearrange("p (c m) -> p c m", c=EC)
        w2s = pv("w2s")
        r1 = pv("r1").rearrange("p (k c m) -> p k c m", k=KD, c=REF // P)
        r2 = pv("r2").rearrange("p (c m) -> p c m", c=REF // P)
        bindm = pv("bind").rearrange("p (k m) -> p k m", k=KD)
        unbindm = pv("unbind").rearrange("p (k m) -> p k m", k=KD)
        identb = sb("identb", [P, P], bf16)
        expandb = sb("expandb", [E, EC, P], bf16)
        sharedb = sb("sharedb", [3 * E + 3, P], bf16)
        b2parts = sb("b2parts", [3 * E + 3, 3 * D], bf16)
        b2half = sb("b2half", [3 * E + 3, 3 * D], bf16)
        mix = sb("mix", [P, KD, D])
        decays = sb("decays", [P, P])
        small = sb("small", [P, 8])
        half, hb2h, dcol, swc, omsw, ebuf = (small[:, i:i + 1] for i in range(6))
        eps_t = sb("eps_t", [P, 1])
        mhalf_t = sb("mhalf_t", [P, 1])
        ib = sb("ib", [P, D])

        xa = [sb(f"xa{s}", [P, D]) for s in range(NS)]
        xT = sb("xT", [P, KD, P])
        sc = sb("sc", [P, P])
        smx = sb("smx", [P, NS])
        nmx = sb("nmx", [P, NS])
        ex = sb("ex", [P, P])
        esum = sb("esum", [P, NS])
        rinv = sb("rinv", [P, 1])
        eT = sb("eT", [P, P])
        h = sb("h", [P, D])
        st = sb("st", [P, 6])
        mv1 = sb("mv1", [P, 2])
        mv2 = sb("mv2", [P, 2])
        vpe1 = sb("vpe1", [P, 1])
        vpe2 = sb("vpe2", [P, 1])
        rs1 = sb("rs1", [P, 1])
        rs2 = sb("rs2", [P, 1])
        xn = sb("xn", [P, D])
        hx = sb("hx", [P, D])
        holo = [sb(f"holo{s}", [P, KD, P]) for s in range(NS)]
        h2 = sb("h2", [P, D])
        xf = [sb(f"xf{s}", [P, D]) for s in range(NS)]
        u0 = [sb(f"u0{s}", [P, D]) for s in range(NS)]
        base = [sb(f"base{s}", [P, D]) for s in range(NS)]
        xfT = sb("xfT", [P, KD, P])
        rh = sb("rh", [HID, P])
        lg = sb("lg", [P, E])
        top = sb("top", [P, 8])
        topi = sb("topi", [P, 8], u32)
        topf = sb("topf", [P, 2])
        dif = sb("dif", [P, 1])
        tw = sb("tw", [P, 1])
        w3 = [sb(f"w3{s}", [P, BR]) for s in range(NS)]
        mask = sb("mask", [P, 2, 3 * E], bf16)
        maskT = [sb(f"maskT{s}", [3 * E, 2, P], bf16) for s in range(NS)]
        mexp = [sb(f"mexp{s}", [P, 2, EC, P], bf16) for s in range(NS)]
        sh1 = sb("sh1", [P, P])
        sh2 = sb("sh2", [P, P])
        ge1 = sb("ge1", [P, EC, P])
        ge2 = sb("ge2", [P, EC, P])
        hm1 = sb("hm1", [P, 2, EC, P])
        hm2 = sb("hm2", [P, 2, EC, P])
        th1 = sb("th1", [P, NS])
        th2 = sb("th2", [P, NS])
        tan1 = [sb(f"tan1{s}", [P, 2, BR, D]) for s in range(NS)]
        tan2 = [sb(f"tan2{s}", [P, 3, BR, D]) for s in range(NS)]
        b2tmp = tan2[0][0:3 * E + 3, :, :, :].rearrange("p a b d -> p a (b d)")
        rb1 = [sb(f"rb1{s}", [P, BR, D]) for s in range(NS)]
        rb2 = [sb(f"rb2{s}", [P, BR, D]) for s in range(NS)]
        pq = sb("pq", [P, BR, 2, D])
        ab = sb("ab", [P, BR, 2, D])
        gw = sb("gw", [P, BR, D])
        sp2 = sb("sp2", [P, BR, D])
        acc = sb("acc", [P, 2, D])
        acc2 = sb("acc2", [P, 2, D])
        nh = sb("nh", [P, 1])
        h2c = sb("h2c", [P, 1])
        hu = sb("hu", [P, D])
        xd = sb("xd", [P, D])
        v1 = [sb(f"v1{s}", [P, D]) for s in range(NS)]
        x1 = [sb(f"x1{s}", [P, D]) for s in range(NS)]
        u1 = [sb(f"u1{s}", [P, D]) for s in range(NS)]
        x1T = sb("x1T", [P, 2 * KD, P])
        t1 = sb("t1", [P, D])
        t2 = sb("t2", [P, D])
        x2 = sb("x2", [P, D])
        x2T = sb("x2T", [P, KD, P])
        rg = sb("rg", [P, REF // P, P])
        yt = sb("yt", [P, D])
        y = [sb(f"y{s}", [P, D]) for s in range(NS)]

        ctl = [ps("ctl0", 1024), ps("ctl1", 1024)]
        pa = ps("pa", 512)
        pb = ps("pb", 512)
        cd = ps("cd", 1024)
        pc, pd = cd[:, 0:512], cd[:, 512:1024]

        par_in = [sem("par_in0"), sem("par_in1")]
        x_in = [sem(f"x_in{s}") for s in range(NS)]
        y_out = [sem(f"y_out{s}") for s in range(NS)]
        pad_zero, set_dve, set_act, set_pe, set_pool = (
            sem(n) for n in ("pad_zero", "set_dve", "set_act", "set_pe", "set_pool"))
        dve_link = sem("dve_link")
        (xT_ps, score_ps, eT_ps, att_ps, xnT_ps, retr_ps, xfT_ps, rh_ps, lg_ps, mT_ps, me_ps, s1_ps, e1_ps,
         halt1_ps, u1_ps, x1T_ps, s2_ps, e2_ps, halt2_ps, u2_ps, x2T_ps, rl1_ps, rl2_ps) = (
            sem(n) for n in ("xT_ps score_ps eT_ps att_ps xnT_ps retr_ps xfT_ps rh_ps lg_ps mT_ps me_ps s1_ps "
                             "e1_ps halt1_ps u1_ps x1T_ps s2_ps e2_ps halt2_ps u2_ps x2T_ps rl1_ps rl2_ps").split())
        (xT_sb, ex_sb, eT_sb, xfT_sb, rh_sb, tw_sb, mT_sb, me_sb, s1_sb, e1_sb, th1_sb, u1_sb, x1T_sb, s2_sb,
         e2_sb, th2_sb, u2_sb, x2T_sb, rg_sb, ln1_sb, ln2_sb) = (
            sem(n) for n in ("xT_sb ex_sb eT_sb xfT_sb rh_sb tw_sb mT_sb me_sb s1_sb e1_sb th1_sb u1_sb x1T_sb "
                             "s2_sb e2_sb th2_sb u2_sb x2T_sb rg_sb ln1_sb ln2_sb").split())
        (smax_v, mv1_v, xn_v, scan_v, mv2_v, xf_v, dif_v, mask_v, w3_v, hm1_v, x1_v, hm2_v, abs1_v, abs2_v,
         x2_v, y_v) = (
            sem(n) for n in ("smax_v mv1_v xn_v scan_v mv2_v xf_v dif_v mask_v w3_v hm1_v x1_v hm2_v abs1_v "
                             "abs2_v x2_v y_v").split())
        vpe1_g, rs1_g, hx_g, vpe2_g, rs2_g, bs_g, base_g = (
            sem(n) for n in "vpe1_g rs1_g hx_g vpe2_g rs2_g bs_g base_g".split())

        block = ctx.enter_context(nc.Block())

        FIRST_FULL = NS + 2
        TURNS = (NT - 2 - FIRST_FULL) // NS

        def run(eng, slot):
            for t in range(-2, FIRST_FULL):
                slot(Tile(t // NS, t % NS))
            with eng.Fori(0, TURNS) as i:
                for r in range(NS):
                    q, s = divmod(FIRST_FULL + r, NS)
                    slot(Tile(i + q, s, FIRST_FULL + r), i * NS + r)
            for t in range(FIRST_FULL + NS * TURNS, NT + 2):
                slot(Tile(t // NS, t % NS))

        @block.sync
        def _(sp):
            sp.dma_start(par[:, 0:NFIRST], params[:, 0:NFIRST]).then_inc(par_in[0], 16)
            sp.wait_ge(pad_zero, 1)

            x_pairs = x.rearrange("(r two) d -> r (two d)", two=DIL)

            def slot(t, k=None):
                z, m = t.at(3), t.at(-2)
                if z.exists():
                    rows = TAIL if z.s == NS - 1 else P
                    passed(sp, att_ps, z, back=NS)
                    src = x_pairs[bass.ds(z.b * (SEQ // DIL) + z.s * P, rows), 0:D]
                    sp.dma_start(xa[z.s][0:rows, :], src).then_inc(x_in[z.s], 16)
                if m.exists():
                    passed(sp, y_v, m)
                    sp.dma_start(out[bass.ds(m.n * P, P), :], y[m.s][:, :]).then_inc(y_out[m.s], 16)

            sp.dma_start(xa[0][:, :], x_pairs[0:P, 0:D]).then_inc(x_in[0], 16)
            sp.dma_start(par[:, NFIRST:NPARAM], params[:, NFIRST:NPARAM]).then_inc(par_in[1], 16)
            run(sp, slot)
            for s in range(NS):
                sp.wait_ge(y_out[s], 16 * BATCH)

        @block.gpsimd
        def _(pool):
            nc.gpsimd.memset(eps_t[:, :], LN_EPS)
            nc.gpsimd.memset(mhalf_t[:, :], -0.5).then_inc(set_pool, 1)
            pool.wait_ge(set_pool, 1)
            pool.wait_ge(par_in[0], 16)
            nc.gpsimd.tensor_tensor(ib[:, :], pv("iw"), pv("rb2"), ALU.mult).then_inc(set_pool, 1)
            pool.wait_ge(set_pool, 2)

            def slot(t, k=None):
                f = t.at(1)
                if not f.exists():
                    return
                passed(pool, mv1_v, f)
                nc.gpsimd.tensor_tensor(vpe1[:, :], mv1[:, 1:2], eps_t[:, :], ALU.add).then_inc(vpe1_g, 1)
                passed(pool, vpe1_g, f)
                nc.gpsimd.tensor_tensor(rs1[:, :], vpe1[:, :], mhalf_t[:, :], ALU.pow).then_inc(rs1_g, 1)
                passed(pool, xn_v, f)
                passed(pool, mv2_v, f, back=1)
                nc.gpsimd.tensor_tensor(hx[:, :], h[:, :], xn[:, :], ALU.add).then_inc(hx_g, 1)
                passed(pool, mv2_v, f)
                nc.gpsimd.tensor_tensor(vpe2[:, :], mv2[:, 1:2], eps_t[:, :], ALU.add).then_inc(vpe2_g, 1)
                passed(pool, vpe2_g, f)
                nc.gpsimd.tensor_tensor(rs2[:, :], vpe2[:, :], mhalf_t[:, :], ALU.pow).then_inc(rs2_g, 1)
                passed(pool, xf_v, f)
                passed(pool, x1_v, f, back=NS)
                nc.gpsimd.tensor_tensor(u0[f.s][:, :], xf[f.s][:, :], pv("mu"), ALU.subtract)
                passed(pool, y_v, f, back=NS)
                nc.gpsimd.tensor_tensor(base[f.s][:, :], h2[:, :], xf[f.s][:, :], ALU.add).then_inc(bs_g, 1)
                passed(pool, bs_g, f)
                nc.gpsimd.tensor_tensor(base[f.s][:, :], base[f.s][:, :], ib[:, :], ALU.add).then_inc(base_g, 1)

            run(pool, slot)

        @block.tensor
        def _(pe):
            mm = nc.tensor.matmul
            pe.wait_ge(par_in[0], 16)
            for i in range(KD):
                for q in range(KD):
                    last = mm(pa[:, i * D:(i + 1) * D], bindm[:, q, i * P:(i + 1) * P], unbindm[:, q, :],
                              start=(q == 0), stop=(q == KD - 1))
            last.then_inc(set_pe, 1)
            pe.wait_ge(set_dve, 1)
            pe.wait_ge(set_act, 1)
            pe.wait_ge(par_in[1], 16)

            def hidden(ps_tile, w, cols, rhs, nk, done):
                for c in range(cols):
                    for q in range(nk):
                        last = mm(ps_tile[:, c * P:(c + 1) * P], w[:, q, c, :], rhs[:, q, :],
                                  start=(q == 0), stop=(q == nk - 1))
                last.then_inc(done, 1)

            def control(dst, lhs, w2, rows, done, j, ncols):
                bias = sharedb[:, :] if j == 0 else rows[:, j - 1, :]
                nb = 3 * E + 3 if j == 0 else 3 * E
                for a in range(0, ncols, 512):
                    z = min(ncols, a + 512)
                    for q, (l, w) in enumerate(zip(lhs, w2)):
                        mm(dst[:, a:z], l, w[:, a:z], start=(q == 0), stop=False)
                    last = mm(dst[:, a:z], bias, b2parts[0:nb, a:z], start=False, stop=True)
                last.then_inc(done, 1)

            def slot(t, k=None):
                f, z, n, m = t.at(1), t.at(2), t.at(-1), t.at(-2)
                w2_chunks = [w2e[:, c, :] for c in range(EC)]
                if t.exists():
                    passed(pe, xfT_sb, t)
                    passed(pe, y_v, t, back=3)
                    passed(pe, th2_sb, t, back=2)
                    for q in range(KD):
                        last = mm(pb[:, 0:P], w1s[:, q, :], xfT[:, q, :], start=(q == 0), stop=(q == KD - 1))
                    last.then_inc(s1_ps, 1)
                    passed(pe, rg_sb, t, back=3)
                    passed(pe, e2_sb, t, back=2)
                    hidden(pa, w1e, EC, xfT, KD, e1_ps)
                if f.exists():
                    passed(pe, ex_sb, f)
                    passed(pe, me_sb, f, back=1)
                    passed(pe, xT_sb, f)
                    nc.tensor.transpose(pc[:, 0:P], ex[:, :], ident).then_inc(eT_ps, 1)
                if t.exists():
                    passed(pe, s1_sb, t)
                    passed(pe, u1_sb, t, back=1, per=BR)
                    passed(pe, u2_sb, t, back=2, per=BR)
                    control(ctl[0], [sh1[:, :]], [w2s], maskT[t.s], u1_ps, 0, 2 * D)
                if f.exists():
                    passed(pe, eT_sb, f)
                    passed(pe, smax_v, f)
                    passed(pe, me_sb, f, back=1)
                    mm(pd[:, 0:D], eT[:, :], xa[f.s][:, :], start=True, stop=True).then_inc(att_ps, 1)
                if t.exists():
                    mm(pb[:, 0:1], sh1[:, :], pv("w2h"), start=True, stop=True).then_inc(halt1_ps, 1)
                    passed(pe, hm1_v, t, back=1, per=2, plus=1)
                    control(ctl[1], [hm1[:, 0, c, :] for c in range(EC)], w2_chunks, maskT[t.s], u1_ps, 1, 2 * D)
                if f.exists():
                    passed(pe, xn_v, f)
                    passed(pe, eT_sb, f)
                    for q in range(KD):
                        last = nc.tensor.transpose(pc[:, q * P:(q + 1) * P], xn[:, q * P:(q + 1) * P], ident)
                    last.then_inc(xnT_ps, 1)
                if t.exists():
                    passed(pe, hm1_v, t, per=2)
                    passed(pe, u1_sb, t, back=1, per=BR, plus=1)
                    control(ctl[0], [hm1[:, 1, c, :] for c in range(EC)], w2_chunks, maskT[t.s], u1_ps, 2, 2 * D)
                if f.exists():
                    passed(pe, scan_v, f)
                    passed(pe, mv1_v, f)
                    for q in range(KD):
                        last = mm(pd[:, 0:D], holo[f.s][:, q, :], mix[:, q, :], start=(q == 0), stop=(q == KD - 1))
                    last.then_inc(retr_ps, 1)
                if n.exists():
                    passed(pe, x1_v, n)
                    if f.exists():
                        passed(pe, scan_v, f)
                    else:
                        passed(pe, me_sb, Tile(BATCH - 1, NS - 1))
                        passed(pe, x2T_sb, n, back=2)
                    for q in range(2 * KD):
                        src = (x1 if q < KD else v1)[n.s][:, (q % KD) * P:(q % KD + 1) * P]
                        last = nc.tensor.transpose(pc[:, q * P:(q + 1) * P], src, ident)
                    last.then_inc(x1T_ps, 1)
                    passed(pe, x1T_sb, n)
                    if t.exists():
                        passed(pe, th1_sb, t)
                        passed(pe, e1_sb, t)
                    else:
                        passed(pe, y_v, n, back=2)
                        passed(pe, rg_sb, n, back=2)
                    for q in range(2 * KD):
                        last = mm(pb[:, 0:P], w1s[:, q, :], x1T[:, q, :], start=(q == 0), stop=(q == 2 * KD - 1))
                    last.then_inc(s2_ps, 1)
                    hidden(pa, w1e, EC, x1T, 2 * KD, e2_ps)
                if z.exists():
                    z_in = 16 * (z.b + 1)
                    pe.wait_ge(x_in[z.s], z_in)
                    if n.exists():
                        passed(pe, x1T_sb, n)
                    if f.exists():
                        passed(pe, scan_v, f)
                    for q in range(KD):
                        last = nc.tensor.transpose(pc[:, q * P:(q + 1) * P], xa[z.s][:, q * P:(q + 1) * P], ident)
                    last.then_inc(xT_ps, 1)
                if n.exists():
                    passed(pe, s2_sb, n)
                    if t.exists():
                        passed(pe, u1_sb, t, back=1, per=BR, plus=2)
                    else:
                        passed(pe, u2_sb, n, back=1, per=BR)
                    control(ctl[1], [sh2[:, :]], [w2s], maskT[n.s], u2_ps, 0, 3 * D)
                if f.exists():
                    passed(pe, xf_v, f)
                    if z.exists():
                        passed(pe, xT_sb, z)
                    elif n.exists():
                        passed(pe, x1T_sb, n)
                    for q in range(KD):
                        last = nc.tensor.transpose(pc[:, q * P:(q + 1) * P], xf[f.s][:, q * P:(q + 1) * P], ident)
                    last.then_inc(xfT_ps, 1)
                if n.exists():
                    mm(pb[:, 0:1], sh2[:, :], pv("w2h"), start=True, stop=True).then_inc(halt2_ps, 1)
                if z.exists():
                    passed(pe, xT_sb, z)
                    if f.exists():
                        passed(pe, mv2_v, f)
                    for q in range(KD):
                        last = mm(pd[:, 0:P], xT[:, q, :], xT[:, q, :], start=(q == 0), stop=(q == KD - 1))
                    last.then_inc(score_ps, 1)
                if n.exists():
                    passed(pe, hm2_v, n, back=1, per=2, plus=1)
                    if t.exists():
                        passed(pe, u1_sb, t, per=BR)
                    control(ctl[0], [hm2[:, 0, c, :] for c in range(EC)], w2_chunks, maskT[n.s], u2_ps, 1, 3 * D)
                if f.exists():
                    passed(pe, xfT_sb, f)
                    if z.exists():
                        passed(pe, smax_v, z)
                    else:
                        passed(pe, mv2_v, f)
                    for q in range(KD):
                        last = mm(pd[0:HID, 0:P], w1r[:, q, :], xfT[:, q, :], start=(q == 0), stop=(q == KD - 1))
                    last.then_inc(rh_ps, 1)
                if m.exists():
                    passed(pe, x2_v, m)
                    if f.exists():
                        passed(pe, xfT_sb, f)
                    elif n.exists():
                        passed(pe, x1T_sb, n)
                    for q in range(KD):
                        last = nc.tensor.transpose(pc[:, q * P:(q + 1) * P], x2[:, q * P:(q + 1) * P], ident)
                    last.then_inc(x2T_ps, 1)
                    passed(pe, x2T_sb, m)
                    if n.exists():
                        passed(pe, e2_sb, n)
                    hidden(pa, r1, REF // P, x2T, KD, rl1_ps)
                if f.exists():
                    passed(pe, rh_sb, f)
                    mm(pd[:, 0:E], rh[:, :], pv("w2r", HID), start=True, stop=True).then_inc(lg_ps, 1)
                if n.exists():
                    passed(pe, hm2_v, n, per=2)
                    passed(pe, u2_sb, n, back=1, per=BR, plus=1)
                    control(ctl[1], [hm2[:, 1, c, :] for c in range(EC)], w2_chunks, maskT[n.s], u2_ps, 2, 3 * D)
                if f.exists():
                    passed(pe, mask_v, f)
                    if m.exists():
                        passed(pe, x2T_sb, m)
                    passed(pe, xfT_sb, f)
                    for j in range(2):
                        last = mm(pc[0:3 * E, j * P:(j + 1) * P], mask[:, j, :], identb[:, :], start=True, stop=True)
                    last.then_inc(mT_ps, 1)
                    passed(pe, mT_sb, f)
                    for j in range(2):
                        for c in range(EC):
                            last = mm(cd[:, (j * EC + c) * P:(j * EC + c + 1) * P], expandb[:, c, :],
                                      maskT[f.s][0:E, j, :], start=True, stop=True)
                    last.then_inc(me_ps, 1)
                if m.exists():
                    passed(pe, rg_sb, m)
                    if n.exists():
                        passed(pe, th2_sb, n)
                    for c in range(REF // P):
                        last = mm(pb[:, 0:D], rg[:, c, :], r2[:, c, :], start=(c == 0), stop=(c == REF // P - 1))
                    last.then_inc(rl2_ps, 1)

            run(pe, slot)

        @block.scalar
        def _(act):
            act.wait_ge(par_in[0], 16)
            nc.scalar.activation(identb[:, :], ident, ACT.Copy)
            nc.scalar.activation(expandb[:, :, :].rearrange("p c m -> p (c m)"), pv("expand", E), ACT.Copy)
            nc.scalar.activation(sharedb[:, :], pv("shared_row", 3 * E + 3), ACT.Copy).then_inc(set_act, 1)
            nc.scalar.activation(dcol, pv("decay"), ACT.Exp, scale=-1.0)
            nc.scalar.activation(swc, pv("sw"), ACT.Exp, scale=-1.0).then_inc(set_act, 1)
            act.wait_ge(set_dve, 1)

            def slot(t, k=None):
                f, z, n, m = t.at(1), t.at(2), t.at(-1), t.at(-2)
                if t.exists():
                    passed(act, s1_ps, t)
                    nc.scalar.activation(sh1[:, :], pb[:, 0:P], ACT.Gelu, bias=pv("b1s")).then_inc(s1_sb, 1)
                    passed(act, e1_ps, t)
                    passed(act, hm1_v, t, back=1, per=2)
                    for c in range(EC):
                        a = OFF["b1e"][0] + c
                        last = nc.scalar.activation(ge1[:, c, :], pa[:, c * P:(c + 1) * P], ACT.Gelu,
                                                    bias=par[:, a:a + 1])
                    last.then_inc(e1_sb, 1)
                if f.exists():
                    passed(act, eT_ps, f)
                    passed(act, att_ps, f, back=1)
                    nc.scalar.activation(eT[:, :], pc[:, 0:P], ACT.Copy).then_inc(eT_sb, 1)

                def unit(tile, j, done, ps_sem, tan, rb, ctl_t, kinds, free):
                    passed(act, ps_sem, tile, back=1, per=BR, plus=j + 1)
                    if j == 0:
                        free()
                    nc.scalar.activation(tan[tile.s][:, 0:kinds, j, :],
                                         ctl_t[:, 0:kinds * D].rearrange("p (a d) -> p a d", a=kinds),
                                         ACT.Tanh, scale=0.5)
                    nc.scalar.activation(rb[tile.s][:, j, :], ctl_t[:, 0:D], ACT.Relu).then_inc(done, 1)

                if t.exists():
                    free1 = lambda: passed(act, x1_v, t, back=2)
                    unit(t, 0, u1_sb, u1_ps, tan1, rb1, ctl[0], 2, free1)
                    passed(act, halt1_ps, t)
                    nc.scalar.activation(th1[:, t.s:t.s + 1], pb[:, 0:1], ACT.Tanh, scale=0.5,
                                         bias=hb2h).then_inc(th1_sb, 1)
                    unit(t, 1, u1_sb, u1_ps, tan1, rb1, ctl[1], 2, free1)
                    unit(t, 2, u1_sb, u1_ps, tan1, rb1, ctl[0], 2, free1)
                if n.exists():
                    passed(act, x1T_ps, n)
                    nc.scalar.activation(x1T[:, :, :].rearrange("p k m -> p (k m)"), pc[:, 0:2 * D],
                                         ACT.Copy).then_inc(x1T_sb, 1)
                    passed(act, s2_ps, n)
                    nc.scalar.activation(sh2[:, :], pb[:, 0:P], ACT.Gelu, bias=pv("b1s")).then_inc(s2_sb, 1)
                    passed(act, e2_ps, n)
                    passed(act, hm2_v, n, back=1, per=2)
                    for c in range(EC):
                        a = OFF["b1e"][0] + c
                        last = nc.scalar.activation(ge2[:, c, :], pa[:, c * P:(c + 1) * P], ACT.Gelu,
                                                    bias=par[:, a:a + 1])
                    last.then_inc(e2_sb, 1)
                if z.exists():
                    passed(act, xT_ps, z)
                    nc.scalar.activation(xT[:, :, :].rearrange("p k m -> p (k m)"), pc[:, 0:D],
                                         ACT.Copy).then_inc(xT_sb, 1)
                free2 = lambda: passed(act, x2_v, n, back=2)
                if n.exists():
                    unit(n, 0, u2_sb, u2_ps, tan2, rb2, ctl[1], 3, free2)
                if f.exists():
                    passed(act, xfT_ps, f)
                    passed(act, e1_ps, f, back=1)
                    nc.scalar.activation(xfT[:, :, :].rearrange("p k m -> p (k m)"), pc[:, 0:D],
                                         ACT.Copy).then_inc(xfT_sb, 1)
                if n.exists():
                    passed(act, halt2_ps, n)
                    nc.scalar.activation(th2[:, n.s:n.s + 1], pb[:, 0:1], ACT.Tanh, scale=0.5,
                                         bias=hb2h).then_inc(th2_sb, 1)
                    unit(n, 1, u2_sb, u2_ps, tan2, rb2, ctl[0], 3, free2)
                if f.exists():
                    passed(act, rh_ps, f)
                    nc.scalar.activation(rh[:, :], pd[0:HID, 0:P], ACT.Gelu, bias=pv("b1r", HID)).then_inc(rh_sb, 1)
                if m.exists():
                    passed(act, x2T_ps, m)
                    nc.scalar.activation(x2T[:, :, :].rearrange("p k m -> p (k m)"), pc[:, 0:D],
                                         ACT.Copy).then_inc(x2T_sb, 1)
                    passed(act, rl1_ps, m)
                    for c in range(REF // P):
                        a = OFF["rb1"][0] + c
                        last = nc.scalar.activation(rg[:, c, :], pa[:, c * P:(c + 1) * P], ACT.Gelu,
                                                    bias=par[:, a:a + 1])
                    last.then_inc(rg_sb, 1)
                if f.exists():
                    passed(act, dif_v, f)
                    nc.scalar.activation(tw[:, :], dif[:, :], ACT.Tanh, scale=0.5).then_inc(tw_sb, 1)
                if n.exists():
                    unit(n, 2, u2_sb, u2_ps, tan2, rb2, ctl[1], 3, free2)
                if f.exists():
                    passed(act, mT_ps, f)
                    passed(act, u2_ps, f, back=NS, per=BR)
                    nc.scalar.activation(maskT[f.s][:, :, :].rearrange("p j m -> p (j m)"), pc[0:3 * E, 0:2 * P],
                                         ACT.Copy).then_inc(mT_sb, 1)
                    passed(act, me_ps, f)
                    passed(act, hm2_v, f, back=NS, per=2)
                    nc.scalar.activation(mexp[f.s][:, :, :, :].rearrange("p j c m -> p (j c m)"), cd[:, :],
                                         ACT.Copy).then_inc(me_sb, 1)
                if t.exists():
                    passed(act, abs1_v, t)
                    nc.scalar.activation(tan1[t.s][:, 0, :, :], tan1[t.s][:, 0, :, :], ACT.Ln, scale=0.5,
                                         bias=half).then_inc(ln1_sb, 1)
                if n.exists():
                    passed(act, abs2_v, n)
                    nc.scalar.activation(tan2[n.s][:, 0, :, :], tan2[n.s][:, 0, :, :], ACT.Ln, scale=0.5,
                                         bias=half).then_inc(ln2_sb, 1)
                if z.exists():
                    passed(act, smax_v, z)
                    passed(act, eT_ps, z, back=1)
                    nc.scalar.activation(ex[:, :], sc[:, :], ACT.Exp, bias=nmx[:, z.s:z.s + 1],
                                         accum_out=esum[:, z.s:z.s + 1]).then_inc(ex_sb, 1)

            run(act, slot)

        @block.vector
        def _(dve):
            V = nc.vector
            links = [0, 0]
            origin = [None]

            def link(ins):
                links[0] += 1
                ins.then_inc(dve_link, 1)
                dve.wait_ge(dve_link, links[0] if origin[0] is None else origin[0] + (links[0] - links[1]))

            def bearer():
                V.tensor_copy(small[:, 6:7], small[:, 7:8])

            V.memset(xa[NS - 1][96:P, :], 0.0).then_inc(pad_zero, 1)
            V.memset(half, 0.5)
            V.memset(decays[:, :], 1.0)
            for s in range(NS):
                link(V.memset(w3[s][:, :], 0.0))
            dve.wait_ge(par_in[0], 16)
            dve.wait_ge(set_act, 2)
            link(V.tensor_scalar(dcol, dcol, 1.0, None, ALU.add))
            link(V.reciprocal(dcol, dcol))
            link(V.tensor_scalar(decays[:, :], decays[:, :], dcol, None, ALU.mult))
            link(V.tensor_scalar(swc, swc, 1.0, None, ALU.add))
            link(V.reciprocal(swc, swc))
            link(V.tensor_scalar(omsw, swc, -1.0, 1.0, ALU.mult, ALU.add))
            for s in range(NS):
                link(V.tensor_copy(w3[s][:, 0:1], swc))
            dve.wait_ge(set_pe, 1)
            link(V.tensor_scalar(mix[:, :, :].rearrange("p k m -> p (k m)"), pa[:, :], pv("gate"), None, ALU.mult))
            dve.wait_ge(par_in[1], 16)
            link(V.tensor_scalar(hb2h, pv("hb2"), 0.5, None, ALU.mult))
            rows = 3 * E + 3
            raw = pv("b2", rows)
            part = [par[0:rows, OFF["part"][0] + i:OFF["part"][0] + i + 1] for i in range(3)]
            src = raw
            for i in range(3):
                link(V.tensor_copy(b2half[:, :], src))
                if i < 2:
                    link(V.tensor_tensor(b2tmp[:, i, :], src, b2half[:, :], ALU.subtract))
                    src = b2tmp[:, i, :]
                if i == 0:
                    link(V.tensor_scalar(b2tmp[:, 2, :], b2half[:, :], part[0], None, ALU.mult))
                else:
                    link(V.scalar_tensor_tensor(b2tmp[:, 2, :], b2half[:, :], part[i], b2tmp[:, 2, :],
                                                ALU.mult, ALU.add))
            link(V.tensor_copy(b2parts[:, :], b2tmp[:, 2, :]))
            V.memset(small[:, 6:8], 0.0).then_inc(set_dve, 1)

            def slot(t, k=None):
                f, z, n, m = t.at(1), t.at(2), t.at(-1), t.at(-2)
                if k is None:
                    origin[0] = None
                else:
                    if not loop_start:
                        loop_start.append(links[0])
                    origin[0] = k * DVE_LINKS + loop_start[0]
                    links[1] = links[0]
                before = links[0]

                if t.exists():
                    passed(dve, e1_sb, t)
                    passed(dve, me_sb, t)
                    passed(dve, u1_ps, t, back=1, per=BR)
                    for j in range(2):
                        V.tensor_tensor(hm1[:, j, :, :], ge1[:, :, :], mexp[t.s][:, j, :, :],
                                        ALU.mult).then_inc(hm1_v, 1)
                if f.exists():
                    passed(dve, ex_sb, f)
                    link(V.reciprocal(rinv[:, :], esum[:, f.s:f.s + 1]))
                    passed(dve, att_ps, f)
                    passed(dve, hx_g, f, back=1)
                    link(V.tensor_scalar(h[:, :], pd[:, 0:D], rinv[:, :], None, ALU.mult))
                    link(V.bn_stats(st[:, :], h[:, :]))
                    passed(dve, rs1_g, f, back=1)
                    bearer()
                    V.bn_aggr(mv1[:, :], st[:, :]).then_inc(mv1_v, 1)
                if n.exists():
                    passed(dve, ln1_sb, n)
                    sp = pq[:, :, 0, :]
                    link(V.tensor_tensor(sp, rb1[n.s][:, :, :], tan1[n.s][:, 0, :, :], ALU.subtract))
                    link(V.scalar_tensor_tensor(pq[:, :, 1, :], tan1[n.s][:, 1, :, :], 1.0, sp, ALU.add, ALU.mult))
                    link(V.tensor_scalar(acc[:, :, :], pq[:, 0, :, :], w3[n.s][:, 0:1], None, ALU.mult))
                    for j in range(1, BR):
                        link(V.scalar_tensor_tensor(acc[:, :, :], pq[:, j, :, :], w3[n.s][:, j:j + 1], acc[:, :, :],
                                                    ALU.mult, ALU.add))
                if f.exists():
                    passed(dve, rs1_g, f)
                    passed(dve, mv1_v, f)
                    passed(dve, xnT_ps, f, back=1)
                    V.tensor_scalar(xn[:, :], h[:, :], mv1[:, 0:1], rs1[:, :], ALU.subtract,
                                    ALU.mult).then_inc(xn_v, 1)
                if n.exists():
                    passed(dve, th1_sb, n)
                    passed(dve, base_g, n)
                    link(V.tensor_scalar(nh[:, :], th1[:, n.s:n.s + 1], -0.5, -0.5, ALU.mult, ALU.add))
                    link(V.tensor_scalar(hu[:, :], u0[n.s][:, :], nh[:, :], None, ALU.mult))
                    V.tensor_tensor(v1[n.s][:, :], acc[:, 0, :], hu[:, :], ALU.mult)
                    link(V.tensor_tensor(xd[:, :], acc[:, 1, :], hu[:, :], ALU.mult))
                    link(V.scalar_tensor_tensor(x1[n.s][:, :], xd[:, :], 0.05, xf[n.s][:, :], ALU.mult, ALU.add))
                    V.tensor_tensor(u1[n.s][:, :], x1[n.s][:, :], pv("mu"), ALU.subtract).then_inc(x1_v, 1)
                if f.exists():
                    passed(dve, xnT_ps, f)
                    for q in range(KD):
                        carry = 0.0 if f.s == 0 else holo[f.s - 1][:, q, P - 1:P]
                        if f.s and q == 0:
                            passed(dve, scan_v, f, back=1)
                        last = V.tensor_tensor_scan(holo[f.s][:, q, :], decays[:, :], pc[:, q * P:(q + 1) * P], carry,
                                                    ALU.mult, ALU.add)
                    last.then_inc(scan_v, 1)
                    passed(dve, retr_ps, f)
                    passed(dve, hx_g, f)
                    passed(dve, base_g, f, back=1)
                    link(V.tensor_tensor(h2[:, :], pd[:, 0:D], hx[:, :], ALU.add))
                    link(V.bn_stats(st[:, :], h2[:, :]))
                    bearer()
                    V.bn_aggr(mv2[:, :], st[:, :]).then_inc(mv2_v, 1)
                if t.exists():
                    passed(dve, u1_sb, t, per=BR)
                    bits = tan1[t.s][:, 0, :, :].bitcast(u32)
                    V.tensor_scalar(bits, bits, 0x7FFFFFFF, None, ALU.bitwise_and).then_inc(abs1_v, 1)
                if m.exists():
                    passed(dve, ln2_sb, m)
                    for j in range(BR):
                        V.tensor_scalar(gw[:, j, :], tan2[m.s][:, 1, j, :], 1.0, w3[m.s][:, j:j + 1], ALU.add, ALU.mult)
                    link(V.tensor_tensor(sp2[:, :, :], rb2[m.s][:, :, :], tan2[m.s][:, 0, :, :], ALU.subtract))
                if f.exists():
                    passed(dve, rs2_g, f)
                    passed(dve, mv2_v, f)
                    V.tensor_scalar(xf[f.s][:, :], h2[:, :], mv2[:, 0:1], rs2[:, :], ALU.subtract,
                                    ALU.mult).then_inc(xf_v, 1)
                if n.exists():
                    passed(dve, e2_sb, n)
                    passed(dve, u2_ps, n, back=1, per=BR)
                    for j in range(2):
                        V.tensor_tensor(hm2[:, j, :, :], ge2[:, :, :], mexp[n.s][:, j, :, :],
                                        ALU.mult).then_inc(hm2_v, 1)
                if m.exists():
                    V.scalar_tensor_tensor(ab[:, :, 0, :], tan2[m.s][:, 2, :, :], 1.0, gw[:, :, :], ALU.add, ALU.mult)
                    link(V.tensor_tensor(ab[:, :, 1, :], sp2[:, :, :], gw[:, :, :], ALU.mult))
                    link(V.tensor_tensor(acc2[:, :, :], ab[:, 0, :, :], ab[:, 1, :, :], ALU.add))
                    link(V.tensor_tensor(acc2[:, :, :], acc2[:, :, :], ab[:, 2, :, :], ALU.add))
                    passed(dve, th2_sb, m)
                    V.tensor_scalar(h2c[:, :], th2[:, m.s:m.s + 1], 0.025, 0.025, ALU.mult, ALU.add)
                    V.scalar_tensor_tensor(t1[:, :], acc2[:, 0, :], 0.5, v1[m.s][:, :], ALU.mult, ALU.mult)
                    link(V.tensor_tensor(t2[:, :], acc2[:, 1, :], u1[m.s][:, :], ALU.mult))
                    link(V.tensor_tensor(t1[:, :], t1[:, :], t2[:, :], ALU.subtract))
                    passed(dve, x2T_ps, m, back=1)
                    V.scalar_tensor_tensor(x2[:, :], t1[:, :], h2c[:, :], x1[m.s][:, :], ALU.mult,
                                           ALU.add).then_inc(x2_v, 1)
                if z.exists():
                    passed(dve, score_ps, z)
                    passed(dve, ex_sb, z, back=1)
                    link(V.tensor_scalar(sc[:, :], pd[:, 0:P], float(D) ** -0.5, None, ALU.mult, ALU.max,
                                         accum_out=smx[:, z.s:z.s + 1]))
                    V.tensor_scalar(nmx[:, z.s:z.s + 1], smx[:, z.s:z.s + 1], -1.0, None,
                                    ALU.mult).then_inc(smax_v, 1)
                if f.exists():
                    passed(dve, lg_ps, f)
                    link(V.tensor_tensor(lg[:, :], pd[:, 0:E], pv("b2r"), ALU.add))
                    bearer()
                    link(V.max(top[:, :], lg[:, :]))
                    passed(dve, tw_sb, f, back=1)
                    V.tensor_tensor(dif[:, :], top[:, 0:1], top[:, 1:2], ALU.subtract).then_inc(dif_v, 1)
                    link(V.max_index(topi[:, :], top[:, :], lg[:, :]))
                    link(V.tensor_copy(topf[:, :], topi[:, 0:2]))
                    passed(dve, mT_ps, f, back=1)
                    for j in range(2):
                        last = V.tensor_scalar(mask[:, j, :], pv("iota"), topf[:, j:j + 1], None, ALU.is_equal)
                    last.then_inc(mask_v, 1)
                    passed(dve, tw_sb, f)
                    V.tensor_scalar(w3[f.s][:, 1:2], tw[:, :], 0.5, 0.5, ALU.mult, ALU.add)
                    link(V.tensor_scalar(w3[f.s][:, 2:3], tw[:, :], -0.5, 0.5, ALU.mult, ALU.add))
                    link(V.tensor_scalar(w3[f.s][:, 1:3], w3[f.s][:, 1:3], omsw, None, ALU.mult))
                if n.exists():
                    passed(dve, u2_sb, n, per=BR)
                    bits = tan2[n.s][:, 0, :, :].bitcast(u32)
                    V.tensor_scalar(bits, bits, 0x7FFFFFFF, None, ALU.bitwise_and).then_inc(abs2_v, 1)
                if m.exists():
                    passed(dve, rl2_ps, m)
                    link(V.tensor_tensor(yt[:, :], pb[:, 0:D], pv("iw"), ALU.mult))
                    passed(dve, base_g, m)
                    if not isinstance(m.b, int) or m.b > 0:
                        dve.wait_ge(y_out[m.s], 16 * m.b)
                    V.tensor_tensor(y[m.s][:, :], yt[:, :], base[m.s][:, :], ALU.add).then_inc(y_v, 1)
                if k is not None:
                    assert links[0] - before == DVE_LINKS, links[0] - before

            loop_start = []

            def slots(t, k=None):
                if k is None and loop_start and links[0] < loop_start[0] + DVE_LINKS * full_slots:
                    links[0] = loop_start[0] + DVE_LINKS * full_slots
                slot(t, k)

            full_slots = NS * TURNS
            run(dve, slots)


def _pack(i):
    import numpy as np
    a = {n: np.zeros((P, w), np.float32) for n, w in _FIRST + _SECOND}
    a["ident"][:] = np.eye(P)
    for c in range(EC):
        for e in range(P // HID):
            a["expand"][c * (P // HID) + e, c * P + e * HID:c * P + (e + 1) * HID] = 1
    a["iota"][:] = np.tile(np.arange(E), 3)
    for r in range(3 * E + 3):
        a["part"][r, r // E if r < 3 * E else r - 3 * E] = 1
    a["shared_row"][3 * E:3 * E + 3] = 1
    turn = (-(np.arange(D)[:, None] + np.arange(D)[None, :])) % D
    for name, key in (("bind", "L0_attn_bind_key"), ("unbind", "L0_attn_unbind_key")):
        a[name][:] = i[key][turn].reshape(KD, P, D).transpose(1, 0, 2).reshape(P, KD * D)
    a["decay"][:] = i["L0_attn_decay"]
    a["gate"][:] = i["L0_attn_gate"]
    f = {k[len("L0_ffn_"):]: v for k, v in i.items() if k.startswith("L0_ffn_")}
    a["sw"][:] = f["shared_weight"]
    chunks = lambda w: w.reshape(-1, P, w.shape[1]).transpose(1, 0, 2)
    a["w1r"][:] = chunks(f["router_w1"]).reshape(P, -1)
    a["b1r"][0:HID, 0] = f["router_b1"]
    a["w2r"][0:HID] = f["router_w2"]
    a["b2r"][:] = f["router_b2"]
    a["mu"][:] = f["mu"]
    a["iw"][:] = f["integration_weight"]
    a["rb2"][:] = f["refine_b2"]
    w1 = f["expert_w1"].transpose(1, 0, 2).reshape(2 * D, E * HID)
    a["w1e"][:] = chunks(w1).reshape(P, -1)
    s = a["w1s"].reshape(P, 2 * KD, P)
    s[:, :, 0:HID] = chunks(f["shared_w1"])
    s[:, 0:KD, HID:P] = chunks(f["halt_w1"])
    order = np.r_[D:3 * D, 0:D]
    a["w2e"][:] = chunks(f["expert_w2"].reshape(E * HID, 3 * D)[:, order]).reshape(P, -1)
    a["w2s"][0:HID] = f["shared_w2"][:, order]
    a["w2h"][HID:P] = f["halt_w2"]
    a["r1"][:] = chunks(f["refine_w1"]).reshape(P, -1)
    a["r2"][:] = chunks(f["refine_w2"]).reshape(P, -1)
    for r in range(3):
        a["b2"][r * E:(r + 1) * E] = f["expert_b2"][:, order]
        a["b2"][3 * E + r] = f["shared_b2"][order]
    a["b1e"][:] = f["expert_b1"].reshape(EC, P).T
    a["b1s"][:, 0] = np.r_[f["shared_b1"], f["halt_b1"]]
    a["rb1"][:] = f["refine_b1"].reshape(REF // P, P).T
    a["hb2"][:] = f["halt_b2"]
    return np.concatenate([a[n] for n, _ in _FIRST + _SECOND], axis=1)


def kernel(**inputs):
    import numpy as _np
    import concourse.bacc as _bacc
    from concourse import mybir as _mybir
    from concourse.bass_utils import run_bass_kernel_spmd as _run

    i = {k: _np.asarray(v) for k, v in inputs.items()}
    arrays = {"x_dram": _np.ascontiguousarray(i["x"].reshape(BATCH * SEQ, D)), "params_dram": _pack(i)}
    nc = _bacc.Bacc("TRN2", target_bir_lowering=False, num_devices=1)
    args = [nc.dram_tensor(n, a.shape, _mybir.dt.from_np(a.dtype), kind="ExternalInput").ap()
            for n, a in arrays.items()]
    out = nc.dram_tensor("out_dram", (NT * P, D), _mybir.dt.float32, kind="ExternalOutput").ap()
    audio_layer(nc, *args, out)
    r = _run(nc, [arrays], core_ids=[0])
    return r.results[0]["out_dram"].reshape(BATCH, NS * P, D)
```

```python
import concourse.bass as bass
from concourse import mybir
from contextlib import ExitStack

P = 128
BATCH, SEQ, D = 8, 750, 256
SEG, DIL = 256, 2
NS = -(-SEQ // SEG)
NT = BATCH * NS
TAIL = (SEQ - (NS - 1) * SEG + DIL - 1) // DIL
E, HID, REF = 8, 64, 512
KD = D // P
EC = E * HID // P
BR = 3
LN_EPS = 1e-5

_KEPT = [[("ident", P), ("iota", 3 * E), ("part", 3), ("decay", 1), ("gate", 1), ("sw", 1), ("b1r", 1),
          ("w2r", E), ("b2r", E), ("mu", D), ("iw", D), ("rb2", D), ("w2h", 1), ("b1e", EC), ("b1s", 1),
          ("rb1", REF // P), ("hb2", 1), ("w1r", KD * HID)],
         [("w1s", 2 * KD * P), ("w1e", 2 * KD * E * HID)],
         [("w2s", 3 * D), ("r1", KD * REF), ("r2", REF // P * D)]]
_STAGED = [[("bind", KD * D), ("unbind", KD * D), ("expand", EC * P), ("shared_row", P), ("b2", 3 * D)],
           [("w2e", EC * 3 * D)]]
_ALL = sum(_KEPT + _STAGED, [])


def _columns(groups):
    return sum(n for group in groups for _, n in group)


def _offsets():
    at, out = 0, {}
    for name, n in _ALL:
        out[name] = (at, n)
        at += n
    return out


OFF = _offsets()
NKEPT, NSTAGED = _columns(_KEPT), _columns(_STAGED)
TAN, RB = BR * BR * D, BR * D
NWORK = NS * (TAN + RB) + 2 * BR * D + 2 * BR * D + 2 * D


class Tile:

    def __init__(self, b, s, low=None):
        self.b, self.s = b, s
        self.n = b * NS + s
        self.low = self.n if low is None else low

    def at(self, k):
        q, s = divmod(self.s + k, NS)
        return Tile(self.b + q, s, self.low + k)

    def exists(self):
        return not isinstance(self.n, int) or 0 <= self.n < NT


def passed(eng, sem, tile, back=0, per=1, step=None):
    step = per if step is None else step
    if tile.low - back < 0:
        assert isinstance(tile.n, int)
        return
    eng.wait_ge(sem, (tile.n - back) * per + step)


DVE_LINKS = 26


def audio_layer(nc, x, params, out):
    fp32, f32r, bf16 = mybir.dt.float32, mybir.dt.float32r, mybir.dt.bfloat16
    u32 = mybir.dt.uint32
    ALU, ACT, AX = mybir.AluOpType, mybir.ActivationFunctionType, mybir.AxisListType
    ctx = ExitStack()
    with ctx:
        def sb(name, shape, dt=fp32):
            return ctx.enter_context(nc.sbuf_tensor(name, shape, dt))

        def ps(name, cols):
            return ctx.enter_context(nc.psum_tensor(name, [P, cols], fp32))

        def sem(name):
            return ctx.enter_context(nc.semaphore(name))

        par = sb("par", [P, NKEPT])
        work = sb("work", [P, NWORK])

        def pv(name, rows=P):
            a, n = OFF[name]
            return par[0:rows, a:a + n]

        def staged(name, rows=P):
            a, n = OFF[name]
            return work[0:rows, a - NKEPT:a - NKEPT + n]

        ident = pv("ident")
        w2s = pv("w2s")
        r2 = pv("r2").rearrange("p (c m) -> p c m", c=REF // P)
        bindm = staged("bind").rearrange("p (k m) -> p k m", k=KD)
        unbindm = staged("unbind").rearrange("p (k m) -> p k m", k=KD)
        w1e = pv("w1e").rearrange("p (k c m) -> p k c m", k=2 * KD, c=EC)
        w1s = pv("w1s").rearrange("p (k c m) -> p k c m", k=2 * KD, c=1)
        w1r = pv("w1r").rearrange("p (k c m) -> p k c m", k=KD, c=1)
        r1 = pv("r1").rearrange("p (k c m) -> p k c m", k=KD, c=REF // P)
        w2e = [sb(f"w2e_{w}", [P, EC, 3 * D], f32r) for w in ("hi", "lo")]
        identb = sb("identb", [P, P], bf16)
        expandb = sb("expandb", [E, EC, P], bf16)
        sharedb = sb("sharedb", [3 * E + 3, P], bf16)
        b2parts = sb("b2parts", [3 * E + 3, 3 * D], bf16)
        b2half = sb("b2half", [3 * E + 3, 3 * D], bf16)
        mix = sb("mix", [P, KD, D])
        decays = sb("decays", [P, P])
        small = sb("small", [P, 8])
        half, hb2h, dcol, swc, omsw, ebuf = (small[:, i:i + 1] for i in range(6))
        eps_t = sb("eps_t", [P, 1])
        mhalf_t = sb("mhalf_t", [P, 1])
        ib = sb("ib", [P, D])

        tan = [work[:, s * TAN:(s + 1) * TAN].rearrange("p (a j d) -> p a j d", a=BR, j=BR)
               for s in range(NS)]
        w0 = NS * TAN
        rb = [work[:, w0 + s * RB:w0 + (s + 1) * RB].rearrange("p (j d) -> p j d", j=BR)
              for s in range(NS)]
        w0 += NS * RB
        pq = work[:, w0:w0 + 2 * BR * D].rearrange("p (j a d) -> p j a d", j=BR, a=2)
        w0 += 2 * BR * D
        gw = work[:, w0:w0 + BR * D].rearrange("p (j d) -> p j d", j=BR)
        w0 += BR * D
        sp2 = work[:, w0:w0 + BR * D].rearrange("p (j d) -> p j d", j=BR)
        w0 += BR * D
        acc = work[:, w0:w0 + 2 * D].rearrange("p (a d) -> p a d", a=2)
        assert w0 + 2 * D == NWORK
        b2tmp = work[0:3 * E + 3, NSTAGED:NSTAGED + 9 * D].rearrange("p (a m) -> p a m", a=3)

        xa = [sb(f"xa{s}", [P, D]) for s in range(NS)]
        xT = sb("xT", [P, KD, P])
        sc = sb("sc", [P, P])
        smx = sb("smx", [P, NS])
        nmx = sb("nmx", [P, NS])
        ex = sb("ex", [P, P])
        esum = sb("esum", [P, NS])
        rinv = sb("rinv", [P, 1])
        eT = sb("eT", [P, P])
        h = sb("h", [P, D])
        st = sb("st", [P, 6])
        mv1 = sb("mv1", [P, 2])
        mv2 = sb("mv2", [P, 2])
        vpe1 = sb("vpe1", [P, 1])
        vpe2 = sb("vpe2", [P, 1])
        rs1 = sb("rs1", [P, 1])
        rs2 = sb("rs2", [P, 1])
        xn = sb("xn", [P, D])
        hx = sb("hx", [P, D])
        holo = [sb(f"holo{s}", [P, KD, P]) for s in range(NS)]
        h2 = sb("h2", [P, D])
        xf = [sb(f"xf{s}", [P, D]) for s in range(NS)]
        u0 = [sb(f"u0{s}", [P, D]) for s in range(NS)]
        base = [sb(f"base{s}", [P, D]) for s in range(NS)]
        xfT = sb("xfT", [P, KD, P])
        rh = sb("rh", [HID, P])
        lg = sb("lg", [P, E])
        top = sb("top", [P, 8])
        topi = sb("topi", [P, 8], u32)
        topf = sb("topf", [P, 2])
        dif = sb("dif", [P, 1])
        tw = sb("tw", [P, 1])
        w3 = [sb(f"w3{s}", [P, BR]) for s in range(NS)]
        mask = sb("mask", [P, 2, 3 * E], bf16)
        maskT = [sb(f"maskT{s}", [3 * E, 2, P], bf16) for s in range(NS)]
        mexp = [sb(f"mexp{s}", [P, 2, EC, P], bf16) for s in range(NS)]
        sh1 = sb("sh1", [P, P])
        sh2 = sb("sh2", [P, P])
        ge = sb("ge", [P, EC, P])
        gh = sb("gh", [P, EC, P], f32r)
        gl = sb("gl", [P, EC, P])
        hm = [sb(f"hm_{w}", [P, 2, EC, P], f32r) for w in ("hi", "lo")]
        th1 = sb("th1", [P, NS])
        th2 = sb("th2", [P, NS])
        nh = sb("nh", [P, 1])
        h2c = sb("h2c", [P, 1])
        v1 = [sb(f"v1{s}", [P, D]) for s in range(NS)]
        x1 = [sb(f"x1{s}", [P, D]) for s in range(NS)]
        x1T = sb("x1T", [P, 2 * KD, P])
        t1 = sb("t1", [P, D])
        t2 = sb("t2", [P, D])
        x2 = sb("x2", [P, D])
        x2T = sb("x2T", [P, KD, P])
        rg = sb("rg", [P, REF // P, P])
        yt = sb("yt", [P, D])
        y = [sb(f"y{s}", [P, D]) for s in range(NS)]

        ctl = [ps("ctl0", 1024), ps("ctl1", 1024)]
        refined = ctl[0][:, 3 * D:4 * D]
        pa = ps("pa", 512)
        pb = ps("pb", 512)
        cd = ps("cd", 1024)
        pc, pd = cd[:, 0:512], cd[:, 512:1024]
        pr = ps("pr", 512) if False else None

        par_in = [sem(f"par_in{i}") for i in range(len(_KEPT))]
        stage_in = [sem(f"stage_in{i}") for i in range(len(_STAGED))]
        x_in = [sem(f"x_in{s}") for s in range(NS)]
        y_out = [sem(f"y_out{s}") for s in range(NS)]
        pad_zero, set_dve, set_act, set_pe, set_pool = (
            sem(n) for n in ("pad_zero", "set_dve", "set_act", "set_pe", "set_pool"))
        dve_link = sem("dve_link")
        (xT_ps, score_ps, eT_ps, att_ps, xnT_ps, retr_ps, xfT_ps, rh_ps, lg_ps, mT_ps, me_ps, s1_ps, e1_ps,
         halt1_ps, u1_ps, x1T_ps, s2_ps, e2_ps, halt2_ps, u2_ps, x2T_ps, rl1_ps, rl2_ps) = (
            sem(n) for n in ("xT_ps score_ps eT_ps att_ps xnT_ps retr_ps xfT_ps rh_ps lg_ps mT_ps me_ps s1_ps "
                             "e1_ps halt1_ps u1_ps x1T_ps s2_ps e2_ps halt2_ps u2_ps x2T_ps rl1_ps rl2_ps").split())
        (xT_sb, ex_sb, eT_sb, xfT_sb, rh_sb, tw_sb, mT_sb, me_sb, s1_sb, e1_sb, th1_sb, u1_sb, x1T_sb, s2_sb,
         e2_sb, th2_sb, u2_sb, x2T_sb, rg_sb, ln1_sb, ln2_sb, gh1_sb, gh2_sb) = (
            sem(n) for n in ("xT_sb ex_sb eT_sb xfT_sb rh_sb tw_sb mT_sb me_sb s1_sb e1_sb th1_sb u1_sb x1T_sb "
                             "s2_sb e2_sb th2_sb u2_sb x2T_sb rg_sb ln1_sb ln2_sb gh1_sb gh2_sb").split())
        (smax_v, mv1_v, xn_v, scan_v, mv2_v, xf_v, dif_v, mask_v, hm1_v, x1_v, hm2_v, abs1_v, abs2_v,
         x2_v, y_v, gl1_v, gl2_v, pq1_v) = (
            sem(n) for n in ("smax_v mv1_v xn_v scan_v mv2_v xf_v dif_v mask_v hm1_v x1_v hm2_v abs1_v "
                             "abs2_v x2_v y_v gl1_v gl2_v pq1_v").split())
        vpe1_g, rs1_g, hx_g, vpe2_g, rs2_g, u0_g, bs_g, base_g, hl1_g, hl2_g = (
            sem(n) for n in "vpe1_g rs1_g hx_g vpe2_g rs2_g u0_g bs_g base_g hl1_g hl2_g".split())

        block = ctx.enter_context(nc.Block())

        FIRST_FULL = 2 * NS
        TURNS = (NT - 2 - FIRST_FULL) // NS

        def run(eng, slot, before={}):
            for t in range(-2, FIRST_FULL):
                if t in before:
                    before[t]()
                slot(Tile(t // NS, t % NS))
            with eng.Fori(0, TURNS) as i:
                for r in range(NS):
                    q, s = divmod(FIRST_FULL + r, NS)
                    slot(Tile(i + q, s, FIRST_FULL + r), i * NS + r)
            for t in range(FIRST_FULL + NS * TURNS, NT + 3):
                slot(Tile(t // NS, t % NS))

        @block.sync
        def _(sp):
            def load(groups, i, dst, first, done):
                a = _columns(groups[0:i])
                z = a + _columns(groups[i:i + 1])
                sp.dma_start(dst[:, a:z], params[:, first + a:first + z]).then_inc(done[i], 16)

            x_pairs = x.rearrange("(r two) d -> r (two d)", two=DIL)
            load(_KEPT, 0, par, 0, par_in)
            sp.dma_start(xa[0][:, :], x_pairs[0:P, 0:D]).then_inc(x_in[0], 16)
            load(_STAGED, 0, work, NKEPT, stage_in)
            load(_KEPT, 1, par, 0, par_in)
            load(_STAGED, 1, work, NKEPT, stage_in)
            load(_KEPT, 2, par, 0, par_in)
            sp.wait_ge(pad_zero, 1)

            def slot(t, k=None):
                z, o = t.at(3), t.at(-3)
                if z.exists():
                    rows = TAIL if z.s == NS - 1 else P
                    passed(sp, att_ps, z, back=NS)
                    src = x_pairs[bass.ds(z.b * (SEQ // DIL) + z.s * P, rows), 0:D]
                    sp.dma_start(xa[z.s][0:rows, :], src).then_inc(x_in[z.s], 16)
                if o.exists():
                    passed(sp, y_v, o)
                    sp.dma_start(out[bass.ds(o.n * P, P), :], y[o.s][:, :]).then_inc(y_out[o.s], 16)

            run(sp, slot)
            for s in range(NS):
                sp.wait_ge(y_out[s], 16 * BATCH)

        @block.gpsimd
        def _(pool):
            TT = nc.gpsimd.tensor_tensor
            nc.gpsimd.memset(eps_t[:, :], LN_EPS)
            nc.gpsimd.memset(mhalf_t[:, :], -0.5).then_inc(set_pool, 1)
            pool.wait_ge(set_pool, 1)
            pool.wait_ge(par_in[0], 16)
            TT(ib[:, :], pv("iw"), pv("rb2"), ALU.mult).then_inc(set_pool, 1)
            pool.wait_ge(set_pool, 2)

            def mask_lo(tile, done, gl_v, read, back):
                passed(pool, gl_v, tile)
                for j in range(2):
                    passed(pool, me_sb, tile, per=2, step=j + 1)
                    passed(pool, read, tile, back=back, per=BR, step=j + 2)
                    TT(hm[1][:, j, :, :], gl[:, :, :], mexp[tile.s][:, j, :, :], ALU.mult).then_inc(done, 1)

            def slot(t, k=None):
                f, n, m = t.at(1), t.at(-1), t.at(-2)
                if t.exists():
                    if m.exists():
                        mask_lo(t, hl1_g, gl1_v, u2_ps, 2)
                    else:
                        mask_lo(t, hl1_g, gl1_v, u1_ps, 1)
                    passed(pool, y_v, t, back=NS)
                    TT(base[t.s][:, :], h2[:, :], xf[t.s][:, :], ALU.add).then_inc(bs_g, 1)
                    passed(pool, bs_g, t)
                    TT(base[t.s][:, :], base[t.s][:, :], ib[:, :], ALU.add).then_inc(base_g, 1)
                if f.exists():
                    passed(pool, mv1_v, f)
                    TT(vpe1[:, :], mv1[:, 1:2], eps_t[:, :], ALU.add).then_inc(vpe1_g, 1)
                    passed(pool, vpe1_g, f)
                    TT(rs1[:, :], vpe1[:, :], mhalf_t[:, :], ALU.pow).then_inc(rs1_g, 1)
                    passed(pool, xn_v, f)
                    passed(pool, mv2_v, f, back=1)
                    TT(hx[:, :], h[:, :], xn[:, :], ALU.add).then_inc(hx_g, 1)
                if n.exists():
                    if t.exists():
                        mask_lo(n, hl2_g, gl2_v, u1_ps, -1)
                    else:
                        mask_lo(n, hl2_g, gl2_v, u2_ps, 1)
                if f.exists():
                    passed(pool, mv2_v, f)
                    TT(vpe2[:, :], mv2[:, 1:2], eps_t[:, :], ALU.add).then_inc(vpe2_g, 1)
                    passed(pool, vpe2_g, f)
                    TT(rs2[:, :], vpe2[:, :], mhalf_t[:, :], ALU.pow).then_inc(rs2_g, 1)
                    passed(pool, xf_v, f)
                    passed(pool, x1_v, f, back=NS)
                    TT(u0[f.s][:, :], xf[f.s][:, :], pv("mu"), ALU.subtract).then_inc(u0_g, 1)

            run(pool, slot)

        @block.tensor
        def _(pe):
            mm = nc.tensor.matmul
            pe.wait_ge(stage_in[0], 16)
            for i in range(KD):
                for q in range(KD):
                    last = mm(pa[:, i * D:(i + 1) * D], bindm[:, q, i * P:(i + 1) * P], unbindm[:, q, :],
                              start=(q == 0), stop=(q == KD - 1))
            last.then_inc(set_pe, 1)
            pe.wait_ge(par_in[0], 16)
            pe.wait_ge(set_dve, 1)
            pe.wait_ge(set_act, 2)

            def hidden(dst, rows, w, cols, rhs, nk, done):
                for c in range(cols):
                    for q in range(nk):
                        last = mm(dst[0:rows, c * P:(c + 1) * P], w[:, q, c, :], rhs[:, q, :],
                                  start=(q == 0), stop=(q == nk - 1))
                last.then_inc(done, 1)

            def shared_control(dst, sh, done, ncols):
                for a in range(0, ncols, 512):
                    z = min(ncols, a + 512)
                    mm(dst[:, a:z], sh[:, :], w2s[:, a:z], start=True, stop=False)
                    last = mm(dst[:, a:z], sharedb[:, :], b2parts[0:3 * E + 3, a:z], start=False, stop=True)
                last.then_inc(done, 1)

            def expert_control(dst, j, tile, lo_ready, done, ncols):
                spans = [(a, min(ncols, a + 512)) for a in range(0, ncols, 512)]
                for a, z in spans:
                    mm(dst[:, a:z], maskT[tile.s][:, j, :], b2parts[0:3 * E, a:z], start=True, stop=False)
                    for c in range(EC):
                        for i in range(2):
                            mm(dst[:, a:z], hm[0][:, j, c, :], w2e[i][:, c, a:z], start=False, stop=False)
                    if a == 0:
                        lo_ready()
                    for c in range(EC):
                        last = mm(dst[:, a:z], hm[1][:, j, c, :], w2e[0][:, c, a:z], start=False,
                                  stop=(c == EC - 1))
                last.then_inc(done, 1)

            def slot(t, k=None):
                z, f, n, m, o = t.at(2), t.at(1), t.at(-1), t.at(-2), t.at(-3)
                if t.exists():
                    if t.low == 0:
                        pe.wait_ge(par_in[2], 16)
                        pe.wait_ge(set_dve, 2)
                    passed(pe, s1_sb, t)
                    if m.exists():
                        passed(pe, u2_sb, m, per=BR, step=2)
                    else:
                        passed(pe, u1_sb, t, back=1, per=BR)
                    shared_control(ctl[0], sh1, u1_ps, 2 * D)
                    passed(pe, mT_sb, t)
                    for j in range(2):
                        for c in range(EC):
                            last = mm(cd[:, (j * EC + c) * P:(j * EC + c + 1) * P], expandb[:, c, :],
                                      maskT[t.s][0:E, j, :], start=True, stop=True)
                        last.then_inc(me_ps, 1)
                if o.exists():
                    passed(pe, rg_sb, o)
                    passed(pe, y_v, o, back=1)
                    for c in range(REF // P):
                        last = mm(refined, rg[:, c, :], r2[:, c, :], start=(c == 0), stop=(c == REF // P - 1))
                    last.then_inc(rl2_ps, 1)
                if f.exists():
                    passed(pe, ex_sb, f)
                    if t.exists():
                        passed(pe, me_sb, t, per=2)
                    else:
                        passed(pe, xT_sb, f)
                    nc.tensor.transpose(pc[:, 0:P], ex[:, :], ident).then_inc(eT_ps, 1)
                if t.exists():
                    mm(pb[:, 0:1], sh1[:, :], pv("w2h"), start=True, stop=True).then_inc(halt1_ps, 1)
                    if t.low == 0:
                        pe.wait_ge(set_dve, 3)
                    passed(pe, hm1_v, t, per=2, step=1)
                    if m.exists():
                        passed(pe, u2_sb, m, per=BR)
                    else:
                        passed(pe, u1_sb, t, back=1, per=BR, step=2)
                    expert_control(ctl[1], 0, t, lambda: passed(pe, hl1_g, t, per=2, step=1), u1_ps, 2 * D)
                if f.exists():
                    passed(pe, eT_sb, f)
                    passed(pe, smax_v, f)
                    mm(pd[:, 0:D], eT[:, :], xa[f.s][:, :], start=True, stop=True).then_inc(att_ps, 1)
                if n.exists():
                    passed(pe, x1_v, n)
                    if f.exists():
                        passed(pe, eT_sb, f)
                    elif t.exists():
                        passed(pe, me_sb, t, per=2)
                    else:
                        passed(pe, x2T_sb, n, back=2)
                    for q in range(2 * KD):
                        src = (x1 if q < KD else v1)[n.s][:, (q % KD) * P:(q % KD + 1) * P]
                        last = nc.tensor.transpose(pc[:, q * P:(q + 1) * P], src, ident)
                    last.then_inc(x1T_ps, 1)
                if t.exists():
                    passed(pe, hm1_v, t, per=2)
                    passed(pe, u1_sb, t, per=BR, step=1)
                    expert_control(ctl[0], 1, t, lambda: passed(pe, hl1_g, t, per=2), u1_ps, 2 * D)
                if z.exists():
                    pe.wait_ge(x_in[z.s], 16 * (z.b + 1))
                    if n.exists():
                        passed(pe, x1T_sb, n)
                    elif f.exists():
                        passed(pe, eT_sb, f)
                    for q in range(KD):
                        last = nc.tensor.transpose(pc[:, q * P:(q + 1) * P], xa[z.s][:, q * P:(q + 1) * P], ident)
                    last.then_inc(xT_ps, 1)
                if n.exists():
                    passed(pe, x1T_sb, n)
                    if t.exists():
                        passed(pe, th1_sb, t)
                    else:
                        passed(pe, th2_sb, n, back=1)
                    hidden(pb, P, w1s, 1, x1T, 2 * KD, s2_ps)
                if z.exists():
                    passed(pe, xT_sb, z)
                    if f.exists():
                        passed(pe, mv1_v, f)
                    for q in range(KD):
                        last = mm(pd[:, 0:P], xT[:, q, :], xT[:, q, :], start=(q == 0), stop=(q == KD - 1))
                    last.then_inc(score_ps, 1)
                if n.exists():
                    if t.exists():
                        passed(pe, e1_sb, t)
                    else:
                        passed(pe, e2_sb, n, back=1)
                    hidden(pa, P, w1e, EC, x1T, 2 * KD, e2_ps)
                if f.exists():
                    passed(pe, xn_v, f)
                    if z.exists():
                        passed(pe, xT_sb, z)
                    elif n.exists():
                        passed(pe, x1T_sb, n)
                    for q in range(KD):
                        last = nc.tensor.transpose(pc[:, q * P:(q + 1) * P], xn[:, q * P:(q + 1) * P], ident)
                    last.then_inc(xnT_ps, 1)
                if n.exists():
                    passed(pe, s2_sb, n)
                    if t.exists():
                        passed(pe, u1_sb, t, per=BR, step=2)
                    else:
                        passed(pe, u2_sb, n, back=1, per=BR)
                    passed(pe, rg_sb, n, back=2)
                    shared_control(ctl[1], sh2, u2_ps, 3 * D)
                    mm(pb[:, 0:1], sh2[:, :], pv("w2h"), start=True, stop=True).then_inc(halt2_ps, 1)
                if f.exists():
                    passed(pe, scan_v, f)
                    if z.exists():
                        passed(pe, smax_v, z)
                    else:
                        passed(pe, mv1_v, f)
                    for q in range(KD):
                        last = mm(pd[:, 0:D], holo[f.s][:, q, :], mix[:, q, :], start=(q == 0), stop=(q == KD - 1))
                    last.then_inc(retr_ps, 1)
                if n.exists():
                    passed(pe, hm2_v, n, per=2, step=1)
                    if t.exists():
                        passed(pe, u1_sb, t, per=BR)
                    else:
                        passed(pe, u2_sb, n, back=1, per=BR, step=2)
                    if o.exists():
                        passed(pe, y_v, o)
                    expert_control(ctl[0], 0, n, lambda: passed(pe, hl2_g, n, per=2, step=1), u2_ps, 3 * D)
                if f.exists():
                    passed(pe, xf_v, f)
                    for q in range(KD):
                        last = nc.tensor.transpose(pc[:, q * P:(q + 1) * P], xf[f.s][:, q * P:(q + 1) * P], ident)
                    last.then_inc(xfT_ps, 1)
                if n.exists():
                    passed(pe, hm2_v, n, per=2)
                    passed(pe, u2_sb, n, per=BR, step=1)
                    expert_control(ctl[1], 1, n, lambda: passed(pe, hl2_g, n, per=2), u2_ps, 3 * D)
                if f.exists():
                    passed(pe, xfT_sb, f)
                    passed(pe, mv2_v, f)
                    hidden(pd, HID, w1r, 1, xfT, KD, rh_ps)
                if m.exists():
                    passed(pe, x2_v, m)
                    if f.exists():
                        passed(pe, xfT_sb, f)
                    elif n.exists():
                        passed(pe, x1T_sb, n)
                    else:
                        passed(pe, x2T_sb, m, back=1)
                    for q in range(KD):
                        last = nc.tensor.transpose(pc[:, q * P:(q + 1) * P], x2[:, q * P:(q + 1) * P], ident)
                    last.then_inc(x2T_ps, 1)
                if f.exists():
                    if f.low == 0:
                        pe.wait_ge(par_in[1], 16)
                    if n.exists():
                        passed(pe, th2_sb, n)
                    else:
                        passed(pe, th1_sb, f, back=1)
                    hidden(pb, P, w1s, 1, xfT, KD, s1_ps)
                    passed(pe, rh_sb, f)
                    mm(pd[:, 0:E], rh[:, :], pv("w2r", HID), start=True, stop=True).then_inc(lg_ps, 1)
                    if n.exists():
                        passed(pe, e2_sb, n)
                    else:
                        passed(pe, e1_sb, f, back=1)
                    hidden(pa, P, w1e, EC, xfT, KD, e1_ps)
                if m.exists():
                    passed(pe, x2T_sb, m)
                    if n.exists():
                        passed(pe, u2_sb, n, per=BR)
                    else:
                        passed(pe, rg_sb, m, back=1)
                    hidden(ctl[1][:, 512:1024], P, r1, REF // P, x2T, KD, rl1_ps)
                if f.exists():
                    passed(pe, mask_v, f)
                    if m.exists():
                        passed(pe, x2T_sb, m)
                    else:
                        passed(pe, xfT_sb, f)
                    for j in range(2):
                        last = mm(pc[0:3 * E, j * P:(j + 1) * P], mask[:, j, :], identb[:, :], start=True, stop=True)
                    last.then_inc(mT_ps, 1)

            run(pe, slot)

        @block.scalar
        def _(act):
            AF = nc.scalar.activation
            act.wait_ge(par_in[0], 16)
            AF(dcol, pv("decay"), ACT.Exp, scale=-1.0)
            AF(swc, pv("sw"), ACT.Exp, scale=-1.0).then_inc(set_act, 1)
            AF(identb[:, :], ident, ACT.Copy)
            act.wait_ge(stage_in[0], 16)
            AF(expandb[:, :, :].rearrange("p c m -> p (c m)"), staged("expand", E), ACT.Copy)
            AF(sharedb[:, :], staged("shared_row", 3 * E + 3), ACT.Copy).then_inc(set_act, 1)
            act.wait_ge(set_dve, 1)

            def split_weight():
                act.wait_ge(stage_in[1], 16)
                AF(w2e[0][:, :, :].rearrange("p c m -> p (c m)"), staged("w2e"), ACT.Copy).then_inc(set_act, 1)
                act.wait_ge(set_dve, 3)

            def state(dst, cols, tile, ps_sem, done, read):
                passed(act, ps_sem, tile)
                passed(act, read, tile, back=1)
                AF(dst[:, :, :].rearrange("p k m -> p (k m)"), pc[:, 0:cols], ACT.Copy).then_inc(done, 1)

            def shared_units(tile, s_ps, s_sb, sh, halt_ps):
                passed(act, s_ps, tile)
                passed(act, halt_ps, tile, back=1)
                AF(sh[:, :], pb[:, 0:P], ACT.Gelu, bias=pv("b1s")).then_inc(s_sb, 1)

            def expert_units(tile, e_ps, e_sb, gh_sb):
                passed(act, e_ps, tile)
                for c in range(EC):
                    a = OFF["b1e"][0] + c
                    last = AF(ge[:, c, :], pa[:, c * P:(c + 1) * P], ACT.Gelu, bias=par[:, a:a + 1])
                last.then_inc(e_sb, 1)
                passed(act, e_sb, tile)
                AF(gh[:, :, :], ge[:, :, :], ACT.Copy).then_inc(gh_sb, 1)

            def unit(tile, j, done, ps_sem, ctl_t, kinds):
                passed(act, ps_sem, tile, per=BR, step=j + 1)
                AF(tan[tile.s][:, 0:kinds, j, :], ctl_t[:, 0:kinds * D].rearrange("p (a d) -> p a d", a=kinds),
                   ACT.Tanh, scale=0.5)
                AF(rb[tile.s][:, j, :], ctl_t[:, 0:D], ACT.Relu).then_inc(done, 1)

            def slot(t, k=None):
                z, f, n, m = t.at(2), t.at(1), t.at(-1), t.at(-2)
                if t.exists():
                    passed(act, hm2_v, t, back=NS, per=2)
                    passed(act, hl2_g, t, back=NS, per=2)
                    for j in range(2):
                        passed(act, me_ps, t, per=2, step=j + 1)
                        AF(mexp[t.s][:, j, :, :].rearrange("p c m -> p (c m)"), cd[:, j * EC * P:(j + 1) * EC * P],
                           ACT.Copy).then_inc(me_sb, 1)
                    passed(act, x2_v, t, back=NS)
                    unit(t, 0, u1_sb, u1_ps, ctl[0], 2)
                if f.exists():
                    passed(act, eT_ps, f)
                    passed(act, att_ps, f, back=1)
                    AF(eT[:, :], pc[:, 0:P], ACT.Copy).then_inc(eT_sb, 1)
                if t.exists():
                    passed(act, halt1_ps, t)
                    AF(th1[:, t.s:t.s + 1], pb[:, 0:1], ACT.Tanh, scale=0.5, bias=hb2h).then_inc(th1_sb, 1)
                    unit(t, 1, u1_sb, u1_ps, ctl[1], 2)
                if n.exists():
                    state(x1T, 2 * D, n, x1T_ps, x1T_sb, e2_ps)
                if z.exists():
                    passed(act, xT_ps, z)
                    AF(xT[:, :, :].rearrange("p k m -> p (k m)"), pc[:, 0:D], ACT.Copy).then_inc(xT_sb, 1)
                if t.exists():
                    unit(t, 2, u1_sb, u1_ps, ctl[0], 2)
                if n.exists():
                    shared_units(n, s2_ps, s2_sb, sh2, halt2_ps)
                    if t.exists():
                        passed(act, hm1_v, t, per=2)
                        passed(act, gl1_v, t)
                    else:
                        passed(act, hm2_v, n, back=1, per=2)
                        passed(act, gl2_v, n, back=1)
                    expert_units(n, e2_ps, e2_sb, gh2_sb)
                nc.scalar.preload_act_table_set("natural_log_exp_and_others")
                if m.exists():
                    passed(act, abs2_v, m)
                    AF(tan[m.s][:, 0, :, :], tan[m.s][:, 0, :, :], ACT.Ln, scale=0.5, bias=half).then_inc(ln2_sb, 1)
                if t.exists():
                    passed(act, abs1_v, t)
                    AF(tan[t.s][:, 0, :, :], tan[t.s][:, 0, :, :], ACT.Ln, scale=0.5, bias=half).then_inc(ln1_sb, 1)
                if z.exists():
                    passed(act, smax_v, z)
                    passed(act, eT_ps, z, back=1)
                    AF(ex[:, :], sc[:, :], ACT.Exp, bias=nmx[:, z.s:z.s + 1],
                       accum_out=esum[:, z.s:z.s + 1]).then_inc(ex_sb, 1)
                nc.scalar.preload_act_table_set("gelu_and_others")
                if n.exists():
                    passed(act, pq1_v, n)
                    unit(n, 0, u2_sb, u2_ps, ctl[1], 3)
                    passed(act, halt2_ps, n)
                    AF(th2[:, n.s:n.s + 1], pb[:, 0:1], ACT.Tanh, scale=0.5, bias=hb2h).then_inc(th2_sb, 1)
                    unit(n, 1, u2_sb, u2_ps, ctl[0], 3)
                if f.exists():
                    state(xfT, D, f, xfT_ps, xfT_sb, e1_ps)
                    passed(act, rh_ps, f)
                    AF(rh[:, :], pd[0:HID, 0:P], ACT.Gelu, bias=pv("b1r", HID)).then_inc(rh_sb, 1)
                if m.exists():
                    state(x2T, D, m, x2T_ps, x2T_sb, rl1_ps)
                if n.exists():
                    unit(n, 2, u2_sb, u2_ps, ctl[1], 3)
                if f.exists():
                    shared_units(f, s1_ps, s1_sb, sh1, halt1_ps)
                    if n.exists():
                        passed(act, hm2_v, n, per=2)
                        passed(act, gl2_v, n)
                    else:
                        passed(act, hm1_v, f, back=1, per=2)
                        passed(act, gl1_v, f, back=1)
                    expert_units(f, e1_ps, e1_sb, gh1_sb)
                if m.exists():
                    passed(act, rl2_ps, m, back=1)
                    passed(act, rl1_ps, m)
                    for c in range(REF // P):
                        a = OFF["rb1"][0] + c
                        last = AF(rg[:, c, :], ctl[1][:, 512 + c * P:512 + (c + 1) * P], ACT.Gelu,
                                  bias=par[:, a:a + 1])
                    last.then_inc(rg_sb, 1)
                if f.exists():
                    passed(act, mT_ps, f)
                    passed(act, u2_ps, f, back=NS, per=BR)
                    AF(maskT[f.s][:, :, :].rearrange("p j m -> p (j m)"), pc[0:3 * E, 0:2 * P],
                       ACT.Copy).then_inc(mT_sb, 1)
                    passed(act, dif_v, f)
                    AF(tw[:, :], dif[:, :], ACT.Tanh, scale=0.5).then_inc(tw_sb, 1)

            run(act, slot, {0: split_weight})

        @block.vector
        def _(dve):
            V = nc.vector
            links = [0, 0]
            origin = [None]

            def link(ins):
                links[0] += 1
                ins.then_inc(dve_link, 1)
                dve.wait_ge(dve_link, links[0] if origin[0] is None else origin[0] + (links[0] - links[1]))

            def bearer():
                V.tensor_copy(small[:, 6:7], small[:, 7:8])

            V.memset(xa[NS - 1][96:P, :], 0.0).then_inc(pad_zero, 1)
            V.memset(half, 0.5)
            V.memset(small[:, 6:8], 0.0)
            V.memset(decays[:, :], 1.0)
            for s in range(NS):
                link(V.memset(w3[s][:, :], 0.0))
            dve.wait_ge(par_in[0], 16)
            dve.wait_ge(set_act, 1)
            link(V.tensor_scalar(dcol, dcol, 1.0, None, ALU.add))
            link(V.reciprocal(dcol, dcol))
            link(V.tensor_scalar(decays[:, :], decays[:, :], dcol, None, ALU.mult))
            link(V.tensor_scalar(swc, swc, 1.0, None, ALU.add))
            link(V.reciprocal(swc, swc))
            link(V.tensor_scalar(omsw, swc, -1.0, 1.0, ALU.mult, ALU.add))
            for s in range(NS):
                link(V.tensor_copy(w3[s][:, 0:1], swc))
            link(V.tensor_scalar(hb2h, pv("hb2"), 0.5, None, ALU.mult))
            dve.wait_ge(set_pe, 1)
            V.tensor_scalar(mix[:, :, :].rearrange("p k m -> p (k m)"), pa[:, :], pv("gate"), None,
                            ALU.mult).then_inc(set_dve, 1)

            def split_biases():
                rows = 3 * E + 3
                part = [par[0:rows, OFF["part"][0] + i:OFF["part"][0] + i + 1] for i in range(3)]
                dve.wait_ge(stage_in[0], 16)
                src = staged("b2", rows)
                for i in range(3):
                    link(V.tensor_copy(b2half[:, :], src))
                    if i < 2:
                        link(V.tensor_tensor(b2tmp[:, i, :], src, b2half[:, :], ALU.subtract))
                        src = b2tmp[:, i, :]
                    if i == 0:
                        link(V.tensor_scalar(b2tmp[:, 2, :], b2half[:, :], part[0], None, ALU.mult))
                    else:
                        link(V.scalar_tensor_tensor(b2tmp[:, 2, :], b2half[:, :], part[i], b2tmp[:, 2, :],
                                                    ALU.mult, ALU.add))
                V.tensor_copy(b2parts[:, :], b2tmp[:, 2, :]).then_inc(set_dve, 1)

            def split_weight():
                dve.wait_ge(stage_in[1], 16)
                dve.wait_ge(set_act, 3)
                flat = [p[:, :, :].rearrange("p c m -> p (c m)") for p in w2e]
                V.tensor_tensor(flat[1], staged("w2e"), flat[0].bitcast(fp32), ALU.subtract).then_inc(set_dve, 1)

            def mask_hi(tile, j, done, read, back):
                passed(dve, me_sb, tile, per=2, step=j + 1)
                passed(dve, read, tile, back=back, per=BR, step=j + 2)
                V.tensor_tensor(hm[0][:, j, :, :], ge[:, :, :], mexp[tile.s][:, j, :, :], ALU.mult).then_inc(done, 1)

            def part_lo(tile, gh_sb, gl_v, read, back):
                passed(dve, gh_sb, tile)
                passed(dve, read, tile, back=back, per=2)
                V.tensor_tensor(gl[:, :, :], ge[:, :, :], gh[:, :, :].bitcast(fp32), ALU.subtract).then_inc(gl_v, 1)

            def slot(t, k=None):
                z, f, n, m, o = t.at(2), t.at(1), t.at(-1), t.at(-2), t.at(-3)
                if k is None:
                    origin[0] = None
                else:
                    if not loop_start:
                        loop_start.append(links[0])
                    origin[0] = k * DVE_LINKS + loop_start[0]
                    links[1] = links[0]
                before = links[0]

                if t.exists():
                    passed(dve, e1_sb, t)
                    for j in range(2):
                        if m.exists():
                            mask_hi(t, j, hm1_v, u2_ps, 2)
                        else:
                            mask_hi(t, j, hm1_v, u1_ps, 1)
                if n.exists():
                    passed(dve, pq1_v, n)
                    link(V.tensor_scalar(acc[:, :, :], pq[:, 0, :, :], w3[n.s][:, 0:1], None, ALU.mult))
                    for j in range(1, BR):
                        link(V.scalar_tensor_tensor(acc[:, :, :], pq[:, j, :, :], w3[n.s][:, j:j + 1], acc[:, :, :],
                                                    ALU.mult, ALU.add))
                    passed(dve, th1_sb, n)
                    link(V.tensor_scalar(nh[:, :], th1[:, n.s:n.s + 1], -0.5, -0.5, ALU.mult, ALU.add))
                    passed(dve, u0_g, n)
                    link(V.tensor_scalar(t1[:, :], u0[n.s][:, :], nh[:, :], None, ALU.mult))
                    V.tensor_tensor(v1[n.s][:, :], acc[:, 0, :], t1[:, :], ALU.mult)
                    link(V.tensor_tensor(t2[:, :], acc[:, 1, :], t1[:, :], ALU.mult))
                    V.scalar_tensor_tensor(x1[n.s][:, :], t2[:, :], 0.05, xf[n.s][:, :], ALU.mult,
                                           ALU.add).then_inc(x1_v, 1)
                if o.exists():
                    passed(dve, rl2_ps, o)
                    link(V.tensor_tensor(yt[:, :], refined, pv("iw"), ALU.mult))
                    passed(dve, base_g, o)
                    if not isinstance(o.b, int) or o.b > 0:
                        dve.wait_ge(y_out[o.s], 16 * o.b)
                    V.tensor_tensor(y[o.s][:, :], yt[:, :], base[o.s][:, :], ALU.add).then_inc(y_v, 1)
                if f.exists():
                    passed(dve, ex_sb, f)
                    link(V.reciprocal(rinv[:, :], esum[:, f.s:f.s + 1]))
                    passed(dve, att_ps, f)
                    passed(dve, hx_g, f, back=1)
                    link(V.tensor_scalar(h[:, :], pd[:, 0:D], rinv[:, :], None, ALU.mult))
                    link(V.bn_stats(st[:, :], h[:, :]))
                    passed(dve, rs1_g, f, back=1)
                    bearer()
                    V.bn_aggr(mv1[:, :], st[:, :]).then_inc(mv1_v, 1)
                if m.exists():
                    passed(dve, u2_sb, m, per=BR)
                    bits = tan[m.s][:, 0, :, :].bitcast(u32)
                    V.tensor_scalar(bits, bits, 0x7FFFFFFF, None, ALU.bitwise_and).then_inc(abs2_v, 1)
                if f.exists():
                    passed(dve, rs1_g, f)
                    passed(dve, mv1_v, f)
                    passed(dve, xnT_ps, f, back=1)
                    V.tensor_scalar(xn[:, :], h[:, :], mv1[:, 0:1], rs1[:, :], ALU.subtract,
                                    ALU.mult).then_inc(xn_v, 1)
                if t.exists():
                    passed(dve, u1_sb, t, per=BR)
                    bits = tan[t.s][:, 0, :, :].bitcast(u32)
                    V.tensor_scalar(bits, bits, 0x7FFFFFFF, None, ALU.bitwise_and).then_inc(abs1_v, 1)
                if z.exists():
                    passed(dve, score_ps, z)
                    passed(dve, ex_sb, z, back=1)
                    link(V.tensor_scalar(sc[:, :], pd[:, 0:P], float(D) ** -0.5, None, ALU.mult, ALU.max,
                                         accum_out=smx[:, z.s:z.s + 1]))
                    V.tensor_scalar(nmx[:, z.s:z.s + 1], smx[:, z.s:z.s + 1], -1.0, None,
                                    ALU.mult).then_inc(smax_v, 1)
                if f.exists():
                    passed(dve, xnT_ps, f)
                    for q in range(KD):
                        carry = 0.0 if f.s == 0 else holo[f.s - 1][:, q, P - 1:P]
                        if f.s and q == 0:
                            passed(dve, scan_v, f, back=1)
                        last = V.tensor_tensor_scan(holo[f.s][:, q, :], decays[:, :], pc[:, q * P:(q + 1) * P], carry,
                                                    ALU.mult, ALU.add)
                    last.then_inc(scan_v, 1)
                if n.exists():
                    passed(dve, e2_sb, n)
                    if t.exists():
                        mask_hi(n, 0, hm2_v, u1_ps, -1)
                        part_lo(n, gh2_sb, gl2_v, hl1_g, -1)
                        mask_hi(n, 1, hm2_v, u1_ps, -1)
                    else:
                        mask_hi(n, 0, hm2_v, u2_ps, 1)
                        part_lo(n, gh2_sb, gl2_v, hl2_g, 1)
                        mask_hi(n, 1, hm2_v, u2_ps, 1)
                if f.exists():
                    passed(dve, retr_ps, f)
                    passed(dve, hx_g, f)
                    passed(dve, base_g, f, back=1)
                    link(V.tensor_tensor(h2[:, :], pd[:, 0:D], hx[:, :], ALU.add))
                    link(V.bn_stats(st[:, :], h2[:, :]))
                    bearer()
                    V.bn_aggr(mv2[:, :], st[:, :]).then_inc(mv2_v, 1)
                if m.exists():
                    passed(dve, ln2_sb, m)
                    for j in range(BR):
                        V.tensor_scalar(gw[:, j, :], tan[m.s][:, 1, j, :], 1.0, w3[m.s][:, j:j + 1], ALU.add, ALU.mult)
                    link(V.tensor_tensor(sp2[:, :, :], rb[m.s][:, :, :], tan[m.s][:, 0, :, :], ALU.subtract))
                if f.exists():
                    passed(dve, rs2_g, f)
                    passed(dve, mv2_v, f)
                    V.tensor_scalar(xf[f.s][:, :], h2[:, :], mv2[:, 0:1], rs2[:, :], ALU.subtract,
                                    ALU.mult).then_inc(xf_v, 1)
                if m.exists():
                    V.scalar_tensor_tensor(pq[:, :, 0, :], tan[m.s][:, 2, :, :], 1.0, gw[:, :, :], ALU.add, ALU.mult)
                    V.tensor_tensor(t2[:, :], x1[m.s][:, :], pv("mu"), ALU.subtract)
                    link(V.tensor_tensor(pq[:, :, 1, :], sp2[:, :, :], gw[:, :, :], ALU.mult))
                    link(V.tensor_tensor(acc[:, :, :], pq[:, 0, :, :], pq[:, 1, :, :], ALU.add))
                    passed(dve, th2_sb, m)
                    V.tensor_scalar(h2c[:, :], th2[:, m.s:m.s + 1], 0.025, 0.025, ALU.mult, ALU.add)
                    link(V.tensor_tensor(acc[:, :, :], acc[:, :, :], pq[:, 2, :, :], ALU.add))
                    V.scalar_tensor_tensor(t1[:, :], acc[:, 0, :], 0.5, v1[m.s][:, :], ALU.mult, ALU.mult)
                    link(V.tensor_tensor(t2[:, :], acc[:, 1, :], t2[:, :], ALU.mult))
                    link(V.tensor_tensor(t1[:, :], t1[:, :], t2[:, :], ALU.subtract))
                    passed(dve, x2T_ps, m, back=1)
                    V.scalar_tensor_tensor(x2[:, :], t1[:, :], h2c[:, :], x1[m.s][:, :], ALU.mult,
                                           ALU.add).then_inc(x2_v, 1)
                if f.exists():
                    passed(dve, lg_ps, f)
                    link(V.tensor_tensor(lg[:, :], pd[:, 0:E], pv("b2r"), ALU.add))
                    bearer()
                    link(V.max(top[:, :], lg[:, :]))
                    passed(dve, tw_sb, f, back=1)
                    V.tensor_tensor(dif[:, :], top[:, 0:1], top[:, 1:2], ALU.subtract).then_inc(dif_v, 1)
                    link(V.max_index(topi[:, :], top[:, :], lg[:, :]))
                    link(V.tensor_copy(topf[:, :], topi[:, 0:2]))
                    passed(dve, mT_ps, f, back=1)
                    for j in range(2):
                        last = V.tensor_scalar(mask[:, j, :], pv("iota"), topf[:, j:j + 1], None, ALU.is_equal)
                    last.then_inc(mask_v, 1)
                if t.exists():
                    passed(dve, ln1_sb, t)
                    sp = pq[:, :, 0, :]
                    link(V.tensor_tensor(sp, rb[t.s][:, :, :], tan[t.s][:, 0, :, :], ALU.subtract))
                    V.scalar_tensor_tensor(pq[:, :, 1, :], tan[t.s][:, 1, :, :], 1.0, sp, ALU.add,
                                           ALU.mult).then_inc(pq1_v, 1)
                if f.exists():
                    if n.exists():
                        part_lo(f, gh1_sb, gl1_v, hl2_g, 2)
                    else:
                        part_lo(f, gh1_sb, gl1_v, hl1_g, 1)
                    passed(dve, tw_sb, f)
                    V.tensor_scalar(w3[f.s][:, 1:2], tw[:, :], 0.5, 0.5, ALU.mult, ALU.add)
                    link(V.tensor_scalar(w3[f.s][:, 2:3], tw[:, :], -0.5, 0.5, ALU.mult, ALU.add))
                    link(V.tensor_scalar(w3[f.s][:, 1:3], w3[f.s][:, 1:3], omsw, None, ALU.mult))
                if k is not None:
                    assert links[0] - before == DVE_LINKS, links[0] - before

            loop_start = []

            def slots(t, k=None):
                if k is None and loop_start and links[0] < loop_start[0] + DVE_LINKS * full_slots:
                    links[0] = loop_start[0] + DVE_LINKS * full_slots
                slot(t, k)

            full_slots = NS * TURNS
            run(dve, slots, {-1: split_biases, 0: split_weight})


def _pack(i):
    import numpy as np
    a = {n: np.zeros((P, w), np.float32) for n, w in _ALL}
    a["ident"][:] = np.eye(P)
    for c in range(EC):
        for e in range(P // HID):
            a["expand"][c * (P // HID) + e, c * P + e * HID:c * P + (e + 1) * HID] = 1
    a["iota"][:] = np.tile(np.arange(E), 3)
    for r in range(3 * E + 3):
        a["part"][r, r // E if r < 3 * E else r - 3 * E] = 1
    a["shared_row"][3 * E:3 * E + 3] = 1
    turn = (-(np.arange(D)[:, None] + np.arange(D)[None, :])) % D
    for name, key in (("bind", "L0_attn_bind_key"), ("unbind", "L0_attn_unbind_key")):
        a[name][:] = i[key][turn].reshape(KD, P, D).transpose(1, 0, 2).reshape(P, KD * D)
    a["decay"][:] = i["L0_attn_decay"]
    a["gate"][:] = i["L0_attn_gate"]
    f = {k[len("L0_ffn_"):]: v for k, v in i.items() if k.startswith("L0_ffn_")}
    a["sw"][:] = f["shared_weight"]
    chunks = lambda w: w.reshape(-1, P, w.shape[1]).transpose(1, 0, 2)
    a["w1r"][:] = chunks(f["router_w1"]).reshape(P, -1)
    a["b1r"][0:HID, 0] = f["router_b1"]
    a["w2r"][0:HID] = f["router_w2"]
    a["b2r"][:] = f["router_b2"]
    a["mu"][:] = f["mu"]
    a["iw"][:] = f["integration_weight"]
    a["rb2"][:] = f["refine_b2"]
    w1 = f["expert_w1"].transpose(1, 0, 2).reshape(2 * D, E * HID)
    a["w1e"][:] = chunks(w1).reshape(P, -1)
    s = a["w1s"].reshape(P, 2 * KD, P)
    s[:, :, 0:HID] = chunks(f["shared_w1"])
    s[:, 0:KD, HID:P] = chunks(f["halt_w1"])
    order = np.r_[D:3 * D, 0:D]
    a["w2e"][:] = chunks(f["expert_w2"].reshape(E * HID, 3 * D)[:, order]).reshape(P, -1)
    a["w2s"][0:HID] = f["shared_w2"][:, order]
    a["w2h"][HID:P] = f["halt_w2"]
    a["r1"][:] = chunks(f["refine_w1"]).reshape(P, -1)
    a["r2"][:] = chunks(f["refine_w2"]).reshape(P, -1)
    for r in range(3):
        a["b2"][r * E:(r + 1) * E] = f["expert_b2"][:, order]
        a["b2"][3 * E + r] = f["shared_b2"][order]
    a["b1e"][:] = f["expert_b1"].reshape(EC, P).T
    a["b1s"][:, 0] = np.r_[f["shared_b1"], f["halt_b1"]]
    a["rb1"][:] = f["refine_b1"].reshape(REF // P, P).T
    a["hb2"][:] = f["halt_b2"]
    return np.concatenate([a[n] for n, _ in _ALL], axis=1)


def kernel(**inputs):
    import numpy as _np
    import concourse.bacc as _bacc
    from concourse import mybir as _mybir
    from concourse.bass_utils import run_bass_kernel_spmd as _run

    i = {k: _np.asarray(v) for k, v in inputs.items()}
    arrays = {"x_dram": _np.ascontiguousarray(i["x"].reshape(BATCH * SEQ, D)), "params_dram": _pack(i)}
    nc = _bacc.Bacc("TRN2", target_bir_lowering=False, num_devices=1)
    args = [nc.dram_tensor(n, a.shape, _mybir.dt.from_np(a.dtype), kind="ExternalInput").ap()
            for n, a in arrays.items()]
    out = nc.dram_tensor("out_dram", (NT * P, D), _mybir.dt.float32, kind="ExternalOutput").ap()
    audio_layer(nc, *args, out)
    r = _run(nc, [arrays], core_ids=[0])
    return r.results[0]["out_dram"].reshape(BATCH, NS * P, D)
```

```python
import concourse.bass as bass
from concourse import mybir
from contextlib import ExitStack

P = 128
BATCH, SEQ, D = 8, 750, 256
SEG, DIL = 256, 2
NS = -(-SEQ // SEG)
NT = BATCH * NS
TAIL = (SEQ - (NS - 1) * SEG + DIL - 1) // DIL
E, HID, REF = 8, 64, 512
KD = D // P
EC = E * HID // P
BR = 3
LN_EPS = 1e-5

_KEPT = [[("ident", P), ("iota", 3 * E), ("part", 4), ("decay", 1), ("gate", 1), ("sw", 1), ("b1r", 1),
          ("w2r", E), ("b2r", E), ("mu", D), ("iw", D), ("rb2", D), ("w2h", 1), ("b1e", EC), ("b1s", 1),
          ("rb1", REF // P), ("hb2", 1), ("w1r", KD * HID)],
         [("w1s", 2 * KD * P), ("w1e", 2 * KD * E * HID)],
         [("r1", KD * REF)]]
_STAGED = [[("bind", KD * D), ("unbind", KD * D)],
           [("expand", EC * P), ("b2", 3 * D), ("w2sa", 3 * D), ("w2sb", 3 * D)],
           [("r2", REF // P * D), ("w2e", EC * 3 * D)]]
_ALL = sum(_KEPT + _STAGED, [])


def _columns(groups):
    return sum(n for group in groups for _, n in group)


def _offsets():
    at, out = 0, {}
    for name, n in _ALL:
        out[name] = (at, n)
        at += n
    return out


OFF = _offsets()
NKEPT, NSTAGED = _columns(_KEPT), _columns(_STAGED)
TAN, RB = BR * BR * D, BR * D
NWORK = NS * (TAN + RB) + 2 * BR * D + 2 * BR * D + 2 * D


class Tile:

    def __init__(self, b, s, low=None):
        self.b, self.s = b, s
        self.n = b * NS + s
        self.low = self.n if low is None else low

    def at(self, k):
        q, s = divmod(self.s + k, NS)
        return Tile(self.b + q, s, self.low + k)

    def exists(self):
        return not isinstance(self.n, int) or 0 <= self.n < NT


def passed(eng, sem, tile, back=0, per=1, step=None):
    step = per if step is None else step
    if tile.low - back < 0:
        assert isinstance(tile.n, int)
        return
    eng.wait_ge(sem, (tile.n - back) * per + step)


HALVES = [slice(0, EC // 2), slice(EC // 2, EC)]
DVE_LINKS = 31


def audio_layer(nc, x, params, out):
    fp32, f32r, bf16 = mybir.dt.float32, mybir.dt.float32r, mybir.dt.bfloat16
    u32 = mybir.dt.uint32
    ALU, ACT = mybir.AluOpType, mybir.ActivationFunctionType
    ctx = ExitStack()
    with ctx:
        def sb(name, shape, dt=fp32):
            return ctx.enter_context(nc.sbuf_tensor(name, shape, dt))

        def ps(name, cols):
            return ctx.enter_context(nc.psum_tensor(name, [P, cols], fp32))

        def sem(name):
            return ctx.enter_context(nc.semaphore(name))

        par = sb("par", [P, NKEPT])
        work = sb("work", [P, NWORK])

        def pv(name, rows=P):
            a, n = OFF[name]
            return par[0:rows, a:a + n]

        def staged(name, rows=P):
            a, n = OFF[name]
            return work[0:rows, a - NKEPT:a - NKEPT + n]

        ident = pv("ident")
        bindm = staged("bind").rearrange("p (k m) -> p k m", k=KD)
        unbindm = staged("unbind").rearrange("p (k m) -> p k m", k=KD)
        w1e = pv("w1e").rearrange("p (k c m) -> p k c m", k=2 * KD, c=EC)
        w1s = pv("w1s").rearrange("p (k c m) -> p k c m", k=2 * KD, c=1)
        w1r = pv("w1r").rearrange("p (k c m) -> p k c m", k=KD, c=1)
        r1 = pv("r1").rearrange("p (k c m) -> p k c m", k=KD, c=REF // P)
        w2e = [sb(f"w2e_{w}", [P, EC, 3 * D], f32r) for w in ("hi", "lo")]
        r2 = [sb(f"r2_{w}", [P, REF // P, D], f32r) for w in ("hi", "lo")]
        SK = HID + 2
        w2sa = sb("w2sa", [P, 3 * D], f32r)
        w2sb = sb("w2sb", [SK, 3 * D], f32r)
        identb = sb("identb", [P, P], bf16)
        expandb = sb("expandb", [E, EC, P], bf16)
        b2parts = sb("b2parts", [3 * E, 3 * D], bf16)
        b2half = sb("b2half", [3 * E, 3 * D], bf16)
        mix = sb("mix", [P, KD, D])
        ones = sb("ones", [P, P])
        decays = sb("decays", [P, P])
        small = sb("small", [P, 8])
        half, hb2h, dcol, swc, omsw = (small[:, i:i + 1] for i in range(5))
        eps_t = sb("eps_t", [P, 1])
        mhalf_t = sb("mhalf_t", [P, 1])
        ib = sb("ib", [P, D])

        tan = [work[:, s * TAN:(s + 1) * TAN].rearrange("p (a j d) -> p a j d", a=BR, j=BR)
               for s in range(NS)]
        w0 = NS * TAN
        rb = [work[:, w0 + s * RB:w0 + (s + 1) * RB].rearrange("p (j d) -> p j d", j=BR)
              for s in range(NS)]
        w0 += NS * RB
        pq = work[:, w0:w0 + 2 * BR * D].rearrange("p (j a d) -> p j a d", j=BR, a=2)
        w0 += 2 * BR * D
        ga = pq.rearrange("p j a d -> p (j a d)")[:, 0:BR * D].rearrange("p (j d) -> p j d", j=BR)
        gw = work[:, w0:w0 + BR * D].rearrange("p (j d) -> p j d", j=BR)
        w0 += BR * D
        sp2 = work[:, w0:w0 + BR * D].rearrange("p (j d) -> p j d", j=BR)
        w0 += BR * D
        acc = work[:, w0:w0 + 2 * D].rearrange("p (a d) -> p a d", a=2)
        assert w0 + 2 * D == NWORK
        spare = work[:, NSTAGED:NSTAGED + 3 * D]

        xa = [sb(f"xa{s}", [P, D]) for s in range(NS)]
        xT = sb("xT", [P, KD, P])
        sc = sb("sc", [P, P])
        smx = sb("smx", [P, NS])
        nmx = sb("nmx", [P, NS])
        ex = sb("ex", [P, P])
        esum = sb("esum", [P, NS])
        rinv = sb("rinv", [P, 1])
        eT = sb("eT", [P, P])
        h = sb("h", [P, D])
        st = sb("st", [P, 6])
        mv1 = sb("mv1", [P, 2])
        mv2 = sb("mv2", [P, 2])
        vpe1 = sb("vpe1", [P, 1])
        vpe2 = sb("vpe2", [P, 1])
        rs1 = sb("rs1", [P, 1])
        rs2 = sb("rs2", [P, 1])
        xn = sb("xn", [P, D])
        hx = sb("hx", [P, D])
        holo = [sb(f"holo{s}", [P, KD, P]) for s in range(NS)]
        h2 = sb("h2", [P, D])
        xf = [sb(f"xf{s}", [P, D]) for s in range(NS)]
        u0 = [sb(f"u0{s}", [P, D]) for s in range(NS)]
        base = [sb(f"base{s}", [P, D]) for s in range(NS)]
        xfT = sb("xfT", [P, KD, P])
        rh = sb("rh", [HID, P])
        lg = sb("lg", [P, E])
        top = sb("top", [P, 8])
        topi = sb("topi", [P, 8], u32)
        topf = sb("topf", [P, 2])
        dif = sb("dif", [P, 1])
        tw = sb("tw", [P, 1])
        w3 = [sb(f"w3{s}", [P, BR]) for s in range(NS)]
        mask = sb("mask", [P, 2, 3 * E], bf16)
        maskT = [sb(f"maskT{s}", [3 * E, 2, P], bf16) for s in range(NS)]
        mexp = [sb(f"mexp{s}", [P, 2, EC, P], bf16) for s in range(NS)]
        sh1 = sb("sh1", [P, P])
        sh2 = sb("sh2", [P, P])
        sa1, sa2 = (sb(f"sa{i}", [P, P], f32r) for i in (1, 2))
        sb1, sb2 = (sb(f"sb{i}", [SK, P], f32r) for i in (1, 2))
        ge = sb("ge", [P, EC, P])
        gh = sb("gh", [P, EC, P], f32r)
        gl = sb("gl", [P, EC, P])
        hm = [sb(f"hm_{w}", [P, 2, EC, P], f32r) for w in ("hi", "lo")]
        th1 = sb("th1", [P, NS])
        th2 = sb("th2", [P, NS])
        nh = sb("nh", [P, 1])
        h2c = sb("h2c", [P, 1])
        v1 = [sb(f"v1{s}", [P, D]) for s in range(NS)]
        x1 = [sb(f"x1{s}", [P, D]) for s in range(NS)]
        x1T = sb("x1T", [P, 2 * KD, P])
        u1 = sb("u1", [P, D])
        t1 = sb("t1", [P, D])
        t2 = sb("t2", [P, D])
        x2 = sb("x2", [P, D])
        x2T = sb("x2T", [P, KD, P])
        rg = sb("rg", [P, REF // P, P])
        rgp = [sb(f"rg_{w}", [P, REF // P, P], f32r) for w in ("hi", "lo")]
        yt = sb("yt", [P, D])
        y = [sb(f"y{s}", [P, D]) for s in range(NS)]

        ctl = [ps("ctl0", 1024), ps("ctl1", 1024)]
        refined = ctl[0][:, 3 * D:4 * D]
        pa = ps("pa", 512)
        pb = ps("pb", 512)
        cd = ps("cd", 1024)
        pc, pd = cd[:, 0:512], cd[:, 512:1024]

        par_in = [sem(f"par_in{i}") for i in range(len(_KEPT))]
        stage_in = [sem(f"stage_in{i}") for i in range(len(_STAGED))]
        x_in = [sem(f"x_in{s}") for s in range(NS)]
        y_out = [sem(f"y_out{s}") for s in range(NS)]
        pad_zero, set_dve, set_act, set_pe, set_pool = (
            sem(n) for n in ("pad_zero", "set_dve", "set_act", "set_pe", "set_pool"))
        dve_link = sem("dve_link")
        (xT_ps, score_ps, eT_ps, att_ps, xnT_ps, retr_ps, xfT_ps, rh_ps, lg_ps, mT_ps, me_ps, s1_ps, e1_ps,
         halt1_ps, u1_ps, x1T_ps, s2_ps, e2_ps, halt2_ps, u2_ps, x2T_ps, rl1_ps, rl2_ps) = (
            sem(n) for n in ("xT_ps score_ps eT_ps att_ps xnT_ps retr_ps xfT_ps rh_ps lg_ps mT_ps me_ps s1_ps "
                             "e1_ps halt1_ps u1_ps x1T_ps s2_ps e2_ps halt2_ps u2_ps x2T_ps rl1_ps rl2_ps").split())
        (xT_sb, ex_sb, eT_sb, xfT_sb, rh_sb, tw_sb, mT_sb, me_sb, s1_sb, e1_sb, th1_sb, u1_sb, x1T_sb, s2_sb,
         e2_sb, th2_sb, u2_sb, x2T_sb, rg_sb, ln1_sb, ln2_sb, gh1_sb, gh2_sb,
         rgh_sb) = (
            sem(n) for n in ("xT_sb ex_sb eT_sb xfT_sb rh_sb tw_sb mT_sb me_sb s1_sb e1_sb th1_sb u1_sb x1T_sb "
                             "s2_sb e2_sb th2_sb u2_sb x2T_sb rg_sb ln1_sb ln2_sb gh1_sb gh2_sb rgh_sb").split())
        (smax_v, mv1_v, xn_v, scan_v, mv2_v, xf_v, dif_v, mask_v, hm1_v, x1_v, hm2_v, abs1_v, abs2_v,
         x2_v, y_v, gl1_v, gl2_v, pq1_v, sl1_v, sl2_v) = (
            sem(n) for n in ("smax_v mv1_v xn_v scan_v mv2_v xf_v dif_v mask_v hm1_v x1_v hm2_v abs1_v "
                             "abs2_v x2_v y_v gl1_v gl2_v pq1_v sl1_v sl2_v").split())
        vpe1_g, rs1_g, hx_g, vpe2_g, rs2_g, u0_g, bs_g, base_g, hl1_g, hl2_g, u1_g, rgl_g = (
            sem(n) for n in "vpe1_g rs1_g hx_g vpe2_g rs2_g u0_g bs_g base_g hl1_g hl2_g u1_g rgl_g".split())

        block = ctx.enter_context(nc.Block())

        FIRST_FULL = 2 * NS
        TURNS = (NT - 2 - FIRST_FULL) // NS

        def run(eng, slot):
            for t in range(-2, FIRST_FULL):
                slot(Tile(t // NS, t % NS))
            with eng.Fori(0, TURNS) as i:
                for r in range(NS):
                    q, s = divmod(FIRST_FULL + r, NS)
                    slot(Tile(i + q, s, FIRST_FULL + r), i * NS + r)
            for t in range(FIRST_FULL + NS * TURNS, NT + 3):
                slot(Tile(t // NS, t % NS))

        @block.sync
        def _(sp):
            def load(groups, i, dst, first, done):
                a = _columns(groups[0:i])
                z = a + _columns(groups[i:i + 1])
                sp.dma_start(dst[:, a:z], params[:, first + a:first + z]).then_inc(done[i], 16)

            x_pairs = x.rearrange("(r two) d -> r (two d)", two=DIL)
            load(_STAGED, 0, work, NKEPT, stage_in)
            load(_KEPT, 0, par, 0, par_in)
            for s in range(2):
                sp.dma_start(xa[s][:, :], x_pairs[s * P:(s + 1) * P, 0:D]).then_inc(x_in[s], 16)
            load(_STAGED, 1, work, NKEPT, stage_in)
            load(_STAGED, 2, work, NKEPT, stage_in)
            load(_KEPT, 1, par, 0, par_in)
            load(_KEPT, 2, par, 0, par_in)
            sp.wait_ge(pad_zero, 1)

            def slot(t, k=None):
                z, o = t.at(3), t.at(-3)
                if z.exists() and z.low > 1:
                    rows = TAIL if z.s == NS - 1 else P
                    passed(sp, att_ps, z, back=NS)
                    src = x_pairs[bass.ds(z.b * (SEQ // DIL) + z.s * P, rows), 0:D]
                    sp.dma_start(xa[z.s][0:rows, :], src).then_inc(x_in[z.s], 16)
                if o.exists():
                    passed(sp, y_v, o)
                    sp.dma_start(out[bass.ds(o.n * P, P), :], y[o.s][:, :]).then_inc(y_out[o.s], 16)

            run(sp, slot)
            for s in range(NS):
                sp.wait_ge(y_out[s], 16 * BATCH)

        @block.gpsimd
        def _(pool):
            TT = nc.gpsimd.tensor_tensor
            nc.gpsimd.memset(eps_t[:, :], LN_EPS)
            nc.gpsimd.memset(mhalf_t[:, :], -0.5).then_inc(set_pool, 1)
            pool.wait_ge(set_pool, 1)
            pool.wait_ge(par_in[0], 16)
            TT(ib[:, :], pv("iw"), pv("rb2"), ALU.mult).then_inc(set_pool, 1)
            pool.wait_ge(set_pool, 2)

            def mask_lo(tile, j, done, gl_v, read, back):
                passed(pool, gl_v, tile)
                passed(pool, me_sb, tile, per=2, step=j + 1)
                passed(pool, read, tile, back=back, per=BR, step=j + 2)
                for c in HALVES if j == 0 else [slice(0, EC)]:
                    TT(hm[1][:, j, c, :], gl[:, c, :], mexp[tile.s][:, j, c, :], ALU.mult).then_inc(done, 1)

            def slot(t, k=None):
                f, n, m, o = t.at(1), t.at(-1), t.at(-2), t.at(-3)
                if t.exists():
                    for j in range(2):
                        mask_lo(t, j, hl1_g, gl1_v, *((u2_ps, 2) if m.exists() else (u1_ps, 1)))
                if o.exists():
                    passed(pool, rgh_sb, o)
                    passed(pool, rl2_ps, o, back=1)
                    TT(rgp[1][:, :, :], rg[:, :, :], rgp[0][:, :, :].bitcast(fp32), ALU.subtract).then_inc(rgl_g, 1)
                if f.exists():
                    passed(pool, mv1_v, f)
                    TT(vpe1[:, :], mv1[:, 1:2], eps_t[:, :], ALU.add).then_inc(vpe1_g, 1)
                    passed(pool, vpe1_g, f)
                    TT(rs1[:, :], vpe1[:, :], mhalf_t[:, :], ALU.pow).then_inc(rs1_g, 1)
                    passed(pool, xn_v, f)
                    passed(pool, mv2_v, f, back=1)
                    TT(hx[:, :], h[:, :], xn[:, :], ALU.add).then_inc(hx_g, 1)
                if m.exists():
                    passed(pool, x1_v, m)
                    passed(pool, x2_v, m, back=1)
                    TT(u1[:, :], x1[m.s][:, :], pv("mu"), ALU.subtract).then_inc(u1_g, 1)
                if t.exists():
                    passed(pool, y_v, t, back=NS)
                    TT(base[t.s][:, :], h2[:, :], xf[t.s][:, :], ALU.add).then_inc(bs_g, 1)
                    passed(pool, bs_g, t)
                    TT(base[t.s][:, :], base[t.s][:, :], ib[:, :], ALU.add).then_inc(base_g, 1)
                if n.exists():
                    after = (u1_ps, -1) if t.exists() else (u2_ps, 1)
                    mask_lo(n, 0, hl2_g, gl2_v, *after)
                if f.exists():
                    passed(pool, mv2_v, f)
                    TT(vpe2[:, :], mv2[:, 1:2], eps_t[:, :], ALU.add).then_inc(vpe2_g, 1)
                    passed(pool, vpe2_g, f)
                    TT(rs2[:, :], vpe2[:, :], mhalf_t[:, :], ALU.pow).then_inc(rs2_g, 1)
                if n.exists():
                    mask_lo(n, 1, hl2_g, gl2_v, *after)
                if f.exists():
                    passed(pool, xf_v, f)
                    passed(pool, x1_v, f, back=NS)
                    TT(u0[f.s][:, :], xf[f.s][:, :], pv("mu"), ALU.subtract).then_inc(u0_g, 1)
                    if f.low == 0:
                        pool.wait_ge(stage_in[2], 16)
                        pool.wait_ge(set_act, 3)
                        for name, w in (("r2", r2), ("w2e", w2e)):
                            flat = [p[:, :, :].rearrange("p c m -> p (c m)") for p in w]
                            last = TT(flat[1], staged(name), flat[0].bitcast(fp32), ALU.subtract)
                        last.then_inc(set_pool, 1)

            run(pool, slot)

        @block.tensor
        def _(pe):
            mm = nc.tensor.matmul
            pe.wait_ge(stage_in[0], 16)
            for i in range(KD):
                for q in range(KD):
                    last = mm(pa[:, i * D:(i + 1) * D], bindm[:, q, i * P:(i + 1) * P], unbindm[:, q, :],
                              start=(q == 0), stop=(q == KD - 1))
            last.then_inc(set_pe, 1)
            pe.wait_ge(par_in[0], 16)

            def hidden(dst, rows, w, chunks, rhs, nk, done=None):
                for c in chunks:
                    for q in range(nk):
                        last = mm(dst[0:rows, c * P:(c + 1) * P], w[:, q, c, :], rhs[:, q, :],
                                  start=(q == 0), stop=(q == nk - 1))
                if done is not None:
                    last.then_inc(done, 1)

            def shared_control(dst, sa, sb, done, ncols):
                for a in range(0, ncols, 512):
                    z = min(ncols, a + 512)
                    mm(dst[:, a:z], sa[:, :], w2sa[:, a:z], start=True, stop=False)
                    last = mm(dst[:, a:z], sb[:, :], w2sb[:, a:z], start=False, stop=True)
                last.then_inc(done, 1)

            def expert_control(dst, j, tile, hi_v, lo_g, done, ncols):
                spans = [(a, min(ncols, a + 512)) for a in range(0, ncols, 512)]
                for a, z in spans:
                    mm(dst[:, a:z], maskT[tile.s][:, j, :], b2parts[0:3 * E, a:z], start=True, stop=False)
                    for c in range(EC):
                        if j == 0 and a == 0 and c == EC // 2:
                            passed(pe, hi_v, tile, per=3, step=2)
                        for i in range(2):
                            mm(dst[:, a:z], hm[0][:, j, c, :], w2e[i][:, c, a:z], start=False, stop=False)
                passed(pe, lo_g, tile, per=3, step=2 * j + 1)
                for a, z in spans:
                    for c in range(EC):
                        if j == 0 and a == 0 and c == EC // 2:
                            passed(pe, lo_g, tile, per=3, step=2)
                        last = mm(dst[:, a:z], hm[1][:, j, c, :], w2e[0][:, c, a:z], start=False,
                                  stop=(c == EC - 1))
                last.then_inc(done, 1)

            def slot(t, k=None):
                z, f, n, m, o = t.at(2), t.at(1), t.at(-1), t.at(-2), t.at(-3)
                if t.exists():
                    passed(pe, s1_sb, t)
                    mm(pb[:, 0:1], sh1[:, :], pv("w2h"), start=True, stop=True).then_inc(halt1_ps, 1)
                    passed(pe, mT_sb, t)
                    for j in range(2):
                        for c in range(EC):
                            last = mm(cd[:, (j * EC + c) * P:(j * EC + c + 1) * P], expandb[:, c, :],
                                      maskT[t.s][0:E, j, :], start=True, stop=True)
                        last.then_inc(me_ps, 1)
                    if t.low == 0:
                        pe.wait_ge(par_in[2], 16)
                        pe.wait_ge(set_dve, 3)
                    passed(pe, sl1_v, t)
                    if m.exists():
                        passed(pe, u2_sb, m, per=BR, step=2)
                    else:
                        passed(pe, u1_sb, t, back=1, per=BR)
                    shared_control(ctl[0], sa1, sb1, u1_ps, 2 * D)
                if o.exists():
                    hidden(ctl[1][:, 512:1024], P, r1, range(EC // 2, EC), x2T, KD, rl1_ps)
                if f.exists():
                    passed(pe, ex_sb, f)
                    if t.exists():
                        passed(pe, me_sb, t, per=2, step=1)
                    else:
                        passed(pe, xT_sb, f)
                    nc.tensor.transpose(pc[:, 0:P], ex[:, :], ident).then_inc(eT_ps, 1)
                if t.exists():
                    if t.low == 0:
                        pe.wait_ge(set_pool, 3)
                    passed(pe, hm1_v, t, per=3, step=1)
                    if m.exists():
                        passed(pe, u2_sb, m, per=BR)
                    else:
                        passed(pe, u1_sb, t, back=1, per=BR, step=2)
                    expert_control(ctl[1], 0, t, hm1_v, hl1_g, u1_ps, 2 * D)
                if f.exists():
                    passed(pe, eT_sb, f)
                    if t.exists():
                        passed(pe, me_sb, t, per=2)
                    else:
                        passed(pe, smax_v, f)
                    mm(pd[:, 0:D], eT[:, :], xa[f.s][:, :], start=True, stop=True).then_inc(att_ps, 1)
                if t.exists():
                    passed(pe, hm1_v, t, per=3)
                    passed(pe, u1_sb, t, per=BR, step=1)
                    expert_control(ctl[0], 1, t, hm1_v, hl1_g, u1_ps, 2 * D)
                if n.exists():
                    passed(pe, x1_v, n)
                    if f.exists():
                        passed(pe, eT_sb, f)
                    elif t.exists():
                        passed(pe, me_sb, t, per=2)
                    else:
                        passed(pe, x2T_sb, n, back=2)
                    for q in range(2 * KD):
                        src = (x1 if q < KD else v1)[n.s][:, (q % KD) * P:(q % KD + 1) * P]
                        last = nc.tensor.transpose(pc[:, q * P:(q + 1) * P], src, ident)
                    last.then_inc(x1T_ps, 1)
                if o.exists():
                    passed(pe, rgl_g, o)
                    passed(pe, y_v, o, back=1)
                    for i, (part, w) in enumerate(((0, 0), (0, 1), (1, 0))):
                        for c in range(REF // P):
                            last = mm(refined, rgp[part][:, c, :], r2[w][:, c, :], start=(i == 0 and c == 0),
                                      stop=(i == 2 and c == REF // P - 1))
                    last.then_inc(rl2_ps, 1)
                if z.exists():
                    pe.wait_ge(x_in[z.s], 16 * (z.b + 1))
                    if n.exists():
                        passed(pe, x1T_sb, n)
                    elif f.exists():
                        passed(pe, eT_sb, f)
                    for q in range(KD):
                        last = nc.tensor.transpose(pc[:, q * P:(q + 1) * P], xa[z.s][:, q * P:(q + 1) * P], ident)
                    last.then_inc(xT_ps, 1)
                if n.exists():
                    passed(pe, x1T_sb, n)
                    if t.exists():
                        passed(pe, th1_sb, t)
                    else:
                        passed(pe, th2_sb, n, back=1)
                    hidden(pb, P, w1s, range(1), x1T, 2 * KD, s2_ps)
                if z.exists():
                    passed(pe, xT_sb, z)
                    if f.exists():
                        passed(pe, mv1_v, f)
                    for q in range(KD):
                        last = mm(pd[:, 0:P], xT[:, q, :], xT[:, q, :], start=(q == 0), stop=(q == KD - 1))
                    last.then_inc(score_ps, 1)
                if f.exists():
                    passed(pe, xn_v, f)
                    if z.exists():
                        passed(pe, xT_sb, z)
                    elif n.exists():
                        passed(pe, x1T_sb, n)
                    for q in range(KD):
                        last = nc.tensor.transpose(pc[:, q * P:(q + 1) * P], xn[:, q * P:(q + 1) * P], ident)
                    last.then_inc(xnT_ps, 1)
                if n.exists():
                    if t.exists():
                        passed(pe, e1_sb, t, per=2)
                    else:
                        passed(pe, e2_sb, n, back=1, per=2)
                    hidden(pa, P, w1e, range(EC), x1T, 2 * KD, e2_ps)
                if n.exists():
                    passed(pe, sl2_v, n)
                    if t.exists():
                        passed(pe, u1_sb, t, per=BR, step=2)
                    else:
                        passed(pe, u2_sb, n, back=1, per=BR)
                    passed(pe, rg_sb, n, back=2)
                    shared_control(ctl[1], sa2, sb2, u2_ps, 3 * D)
                    mm(pb[:, 0:1], sh2[:, :], pv("w2h"), start=True, stop=True).then_inc(halt2_ps, 1)
                if f.exists():
                    if f.low == 0:
                        pe.wait_ge(set_dve, 1)
                    passed(pe, scan_v, f)
                    if z.exists():
                        passed(pe, smax_v, z)
                    else:
                        passed(pe, mv1_v, f)
                    for q in range(KD):
                        last = mm(pd[:, 0:D], holo[f.s][:, q, :], mix[:, q, :], start=(q == 0), stop=(q == KD - 1))
                    last.then_inc(retr_ps, 1)
                if n.exists():
                    passed(pe, hm2_v, n, per=3, step=1)
                    if t.exists():
                        passed(pe, u1_sb, t, per=BR)
                    else:
                        passed(pe, u2_sb, n, back=1, per=BR, step=2)
                    if o.exists():
                        passed(pe, y_v, o)
                    expert_control(ctl[0], 0, n, hm2_v, hl2_g, u2_ps, 3 * D)
                if f.exists():
                    passed(pe, xf_v, f)
                    for q in range(KD):
                        last = nc.tensor.transpose(pc[:, q * P:(q + 1) * P], xf[f.s][:, q * P:(q + 1) * P], ident)
                    last.then_inc(xfT_ps, 1)
                if n.exists():
                    passed(pe, hm2_v, n, per=3)
                    passed(pe, u2_sb, n, per=BR, step=1)
                    expert_control(ctl[1], 1, n, hm2_v, hl2_g, u2_ps, 3 * D)
                if f.exists():
                    passed(pe, xfT_sb, f)
                    passed(pe, mv2_v, f)
                    hidden(pd, HID, w1r, range(1), xfT, KD, rh_ps)
                if m.exists():
                    passed(pe, x2_v, m)
                    if f.exists():
                        passed(pe, xfT_sb, f)
                    elif n.exists():
                        passed(pe, x1T_sb, n)
                    else:
                        passed(pe, x2T_sb, m, back=1)
                    for q in range(KD):
                        last = nc.tensor.transpose(pc[:, q * P:(q + 1) * P], x2[:, q * P:(q + 1) * P], ident)
                    last.then_inc(x2T_ps, 1)
                if f.exists():
                    if f.low == 0:
                        pe.wait_ge(par_in[1], 16)
                    if n.exists():
                        passed(pe, th2_sb, n)
                    else:
                        passed(pe, th1_sb, f, back=1)
                    hidden(pb, P, w1s, range(1), xfT, KD, s1_ps)
                    if n.exists():
                        passed(pe, e2_sb, n, per=2)
                    else:
                        passed(pe, e1_sb, f, back=1, per=2)
                    hidden(pa, P, w1e, range(1), xfT, KD)
                    passed(pe, rh_sb, f)
                    mm(pd[:, 0:E], rh[:, :], pv("w2r", HID), start=True, stop=True).then_inc(lg_ps, 1)
                    hidden(pa, P, w1e, range(1, EC), xfT, KD, e1_ps)
                if m.exists():
                    passed(pe, x2T_sb, m)
                    if n.exists():
                        passed(pe, u2_sb, n, per=BR)
                    else:
                        passed(pe, rg_sb, m, back=1)
                    hidden(ctl[1][:, 512:1024], P, r1, range(1), x2T, KD)
                if f.exists():
                    if f.low == 0:
                        pe.wait_ge(set_act, 2)
                    passed(pe, mask_v, f)
                    if m.exists():
                        passed(pe, x2T_sb, m)
                    else:
                        passed(pe, xfT_sb, f)
                    for j in range(2):
                        last = mm(pc[0:3 * E, j * P:(j + 1) * P], mask[:, j, :], identb[:, :], start=True, stop=True)
                    last.then_inc(mT_ps, 1)
                if m.exists():
                    hidden(ctl[1][:, 512:1024], P, r1, range(1, EC // 2), x2T, KD)

            run(pe, slot)

        @block.scalar
        def _(act):
            AF = nc.scalar.activation
            act.wait_ge(par_in[0], 16)
            AF(dcol, pv("decay"), ACT.Exp, scale=-1.0)
            AF(swc, pv("sw"), ACT.Exp, scale=-1.0).then_inc(set_act, 1)

            def constants():
                AF(identb[:, :], ident, ACT.Copy)
                act.wait_ge(stage_in[1], 16)
                AF(expandb[:, :, :].rearrange("p c m -> p (c m)"), staged("expand", E), ACT.Copy)
                AF(w2sa[:, :], staged("w2sa"), ACT.Copy)
                AF(w2sb[:, :], staged("w2sb", SK), ACT.Copy).then_inc(set_act, 1)

            def state(dst, cols, tile, ps_sem, done, read):
                passed(act, ps_sem, tile)
                passed(act, read, tile, back=1)
                AF(dst[:, :, :].rearrange("p k m -> p (k m)"), pc[:, 0:cols], ACT.Copy).then_inc(done, 1)

            def shared_units(tile, s_ps, s_sb, sh, sa, sb, halt_ps, sl_v):
                passed(act, s_ps, tile)
                passed(act, halt_ps, tile, back=1)
                passed(act, sl_v, tile, back=1)
                AF(sh[:, :], pb[:, 0:P], ACT.Gelu, bias=pv("b1s"))
                AF(sa[0:HID, :], pb[0:HID, 0:P], ACT.Gelu, bias=pv("b1s", HID))
                AF(sb[0:HID, :], pb[0:HID, 0:P], ACT.Gelu, bias=pv("b1s", HID)).then_inc(s_sb, 1)

            def expert_units(tile, e_ps, e_sb):
                passed(act, e_ps, tile)
                for c in range(EC):
                    a = OFF["b1e"][0] + c
                    last = AF(ge[:, c, :], pa[:, c * P:(c + 1) * P], ACT.Gelu, bias=par[:, a:a + 1])
                    if c % (EC // 2) == EC // 2 - 1:
                        last.then_inc(e_sb, 1)

            def hi_part(tile, e_sb, gh_sb):
                passed(act, e_sb, tile, per=2)
                AF(gh[:, :, :], ge[:, :, :], ACT.Copy).then_inc(gh_sb, 1)

            def unit(tile, j, done, ps_sem, ctl_t, kinds):
                passed(act, ps_sem, tile, per=BR, step=j + 1)
                AF(tan[tile.s][:, 0:kinds, j, :], ctl_t[:, 0:kinds * D].rearrange("p (a d) -> p a d", a=kinds),
                   ACT.Tanh, scale=0.5)
                AF(rb[tile.s][:, j, :], ctl_t[:, 0:D], ACT.Relu).then_inc(done, 1)

            def slot(t, k=None):
                z, f, n, m, o = t.at(2), t.at(1), t.at(-1), t.at(-2), t.at(-3)
                if t.exists():
                    passed(act, hm2_v, t, back=NS, per=3)
                    passed(act, hl2_g, t, back=NS, per=3)
                    for j in range(2):
                        passed(act, me_ps, t, per=2, step=j + 1)
                        AF(mexp[t.s][:, j, :, :].rearrange("p c m -> p (c m)"), cd[:, j * EC * P:(j + 1) * EC * P],
                           ACT.Copy).then_inc(me_sb, 1)
                        if j == 0:
                            hi_part(t, e1_sb, gh1_sb)
                    passed(act, dif_v, t)
                    AF(tw[:, :], dif[:, :], ACT.Tanh, scale=0.5).then_inc(tw_sb, 1)
                    if t.low == 0:
                        act.wait_ge(set_dve, 3)
                        act.wait_ge(set_pool, 3)
                    passed(act, x2_v, t, back=NS)
                    unit(t, 0, u1_sb, u1_ps, ctl[0], 2)
                if f.exists():
                    passed(act, eT_ps, f)
                    passed(act, att_ps, f, back=1)
                    AF(eT[:, :], pc[:, 0:P], ACT.Copy).then_inc(eT_sb, 1)
                    if f.low == 0:
                        constants()
                if t.exists():
                    passed(act, halt1_ps, t)
                    AF(th1[:, t.s:t.s + 1], pb[:, 0:1], ACT.Tanh, scale=0.5, bias=hb2h).then_inc(th1_sb, 1)
                if o.exists():
                    passed(act, rl1_ps, o)
                    passed(act, rgl_g, o, back=1)
                    for c in range(REF // P):
                        a = OFF["rb1"][0] + c
                        last = AF(rg[:, c, :], ctl[1][:, 512 + c * P:512 + (c + 1) * P], ACT.Gelu,
                                  bias=par[:, a:a + 1])
                    last.then_inc(rg_sb, 1)
                    passed(act, rg_sb, o)
                    passed(act, rl2_ps, o, back=1)
                    AF(rgp[0][:, :, :], rg[:, :, :], ACT.Copy).then_inc(rgh_sb, 1)
                if t.exists():
                    unit(t, 1, u1_sb, u1_ps, ctl[1], 2)
                if t.exists():
                    unit(t, 2, u1_sb, u1_ps, ctl[0], 2)
                if n.exists():
                    state(x1T, 2 * D, n, x1T_ps, x1T_sb, e2_ps)
                if z.exists():
                    passed(act, xT_ps, z)
                    AF(xT[:, :, :].rearrange("p k m -> p (k m)"), pc[:, 0:D], ACT.Copy).then_inc(xT_sb, 1)
                if n.exists():
                    shared_units(n, s2_ps, s2_sb, sh2, sa2, sb2, halt2_ps, sl2_v)
                    if t.exists():
                        passed(act, hm1_v, t, per=3)
                        passed(act, gl1_v, t)
                    else:
                        passed(act, hm2_v, n, back=1, per=3)
                        passed(act, gl2_v, n, back=1)
                    expert_units(n, e2_ps, e2_sb)
                    hi_part(n, e2_sb, gh2_sb)
                    passed(act, pq1_v, n)
                    unit(n, 0, u2_sb, u2_ps, ctl[1], 3)
                nc.scalar.preload_act_table_set("natural_log_exp_and_others")
                if m.exists():
                    passed(act, abs2_v, m)
                    AF(tan[m.s][:, 0, :, :], tan[m.s][:, 0, :, :], ACT.Ln, scale=0.5, bias=half).then_inc(ln2_sb, 1)
                if t.exists():
                    passed(act, abs1_v, t)
                    AF(tan[t.s][:, 0, :, :], tan[t.s][:, 0, :, :], ACT.Ln, scale=0.5, bias=half).then_inc(ln1_sb, 1)
                if z.exists():
                    passed(act, smax_v, z)
                    passed(act, eT_ps, z, back=1)
                    AF(ex[:, :], sc[:, :], ACT.Exp, bias=nmx[:, z.s:z.s + 1],
                       accum_out=esum[:, z.s:z.s + 1]).then_inc(ex_sb, 1)
                nc.scalar.preload_act_table_set("gelu_and_others")
                if f.exists() and f.low == 0:
                    act.wait_ge(stage_in[2], 16)
                    AF(r2[0][:, :, :].rearrange("p c m -> p (c m)"), staged("r2"), ACT.Copy)
                    AF(w2e[0][:, :, :].rearrange("p c m -> p (c m)"), staged("w2e"), ACT.Copy).then_inc(set_act, 1)
                if n.exists():
                    passed(act, halt2_ps, n)
                    AF(th2[:, n.s:n.s + 1], pb[:, 0:1], ACT.Tanh, scale=0.5, bias=hb2h).then_inc(th2_sb, 1)
                    unit(n, 1, u2_sb, u2_ps, ctl[0], 3)
                if f.exists():
                    state(xfT, D, f, xfT_ps, xfT_sb, e1_ps)
                if f.exists():
                    passed(act, rh_ps, f)
                    AF(rh[:, :], pd[0:HID, 0:P], ACT.Gelu, bias=pv("b1r", HID)).then_inc(rh_sb, 1)
                if m.exists():
                    state(x2T, D, m, x2T_ps, x2T_sb, rl1_ps)
                if n.exists():
                    unit(n, 2, u2_sb, u2_ps, ctl[1], 3)
                if f.exists():
                    shared_units(f, s1_ps, s1_sb, sh1, sa1, sb1, halt1_ps, sl1_v)
                if f.exists():
                    passed(act, mT_ps, f)
                    passed(act, u2_ps, f, back=NS, per=BR)
                    AF(maskT[f.s][:, :, :].rearrange("p j m -> p (j m)"), pc[0:3 * E, 0:2 * P],
                       ACT.Copy).then_inc(mT_sb, 1)
                    if n.exists():
                        passed(act, hm2_v, n, per=3)
                        passed(act, gl2_v, n)
                    else:
                        passed(act, hm1_v, f, back=1, per=3)
                        passed(act, gl1_v, f, back=1)
                    expert_units(f, e1_ps, e1_sb)

            run(act, slot)

        @block.vector
        def _(dve):
            V = nc.vector
            links = [0, 0]
            origin = [None]

            def link(ins):
                links[0] += 1
                ins.then_inc(dve_link, 1)
                dve.wait_ge(dve_link, links[0] if origin[0] is None else origin[0] + (links[0] - links[1]))

            def bearer():
                V.tensor_copy(small[:, 6:7], small[:, 7:8])

            V.memset(xa[NS - 1][96:P, :], 0.0).then_inc(pad_zero, 1)
            V.memset(half, 0.5)
            V.memset(small[:, 6:8], 0.0)
            V.memset(decays[:, :], 1.0)
            V.memset(ones[:, :], 1.0)
            for s in range(NS):
                link(V.memset(w3[s][:, :], 0.0))
            dve.wait_ge(par_in[0], 16)
            dve.wait_ge(set_act, 1)
            link(V.tensor_scalar(dcol, dcol, 1.0, None, ALU.add))
            link(V.reciprocal(dcol, dcol))
            link(V.tensor_scalar(decays[:, :], decays[:, :], dcol, None, ALU.mult))
            link(V.tensor_scalar(swc, swc, 1.0, None, ALU.add))
            link(V.reciprocal(swc, swc))
            link(V.tensor_scalar(omsw, swc, -1.0, 1.0, ALU.mult, ALU.add))
            for s in range(NS):
                link(V.tensor_copy(w3[s][:, 0:1], swc))
            link(V.tensor_scalar(hb2h, pv("hb2"), 0.5, None, ALU.mult))
            for s in (sb1, sb2):
                V.tensor_copy(s[HID:SK, :], ones[HID:SK, :])
            dve.wait_ge(set_pe, 1)
            V.tensor_scalar(mix[:, :, :].rearrange("p k m -> p (k m)"), pa[:, :], pv("gate"), None,
                            ALU.mult).then_inc(set_dve, 1)
            part = [par[:, OFF["part"][0] + i:OFF["part"][0] + i + 1] for i in range(4)]

            def split_biases():
                rows = 3 * E
                dve.wait_ge(stage_in[1], 16)
                src = staged("b2", rows)
                for i in range(2):
                    link(V.tensor_copy(b2half[:, :], src))
                    link(V.scalar_tensor_tensor(spare[0:rows, :], b2half[:, :], part[i][0:rows, :], src,
                                                ALU.mult, ALU.add))
                    src = spare[0:rows, :]
                V.tensor_copy(b2parts[:, :], src).then_inc(set_dve, 1)

            def split_shared():
                dve.wait_ge(set_act, 2)
                link(V.tensor_tensor(spare[0:SK, :], staged("w2sb", SK), w2sb[:, :].bitcast(fp32), ALU.subtract))
                link(V.tensor_scalar(spare[0:SK, :], spare[0:SK, :], part[3][0:SK, :], None, ALU.mult))
                V.scalar_tensor_tensor(w2sb[:, :], w2sb[:, :].bitcast(fp32), part[2][0:SK, :], spare[0:SK, :],
                                       ALU.mult, ALU.add).then_inc(set_dve, 1)

            def shared_lo(tile, s_sb, sh, sa, done):
                passed(dve, s_sb, tile)
                V.tensor_tensor(sa[HID:P, :], sh[0:HID, :], sa[0:HID, :].bitcast(fp32), ALU.subtract).then_inc(done, 1)

            def magnitude(tile, u_sb, done):
                passed(dve, u_sb, tile, per=BR)
                bits = tan[tile.s][:, 0, :, :].bitcast(u32)
                V.tensor_scalar(bits, bits, 0x7FFFFFFF, None, ALU.bitwise_and).then_inc(done, 1)

            def mask_hi(tile, j, e_sb, done, read, back):
                passed(dve, me_sb, tile, per=2, step=j + 1)
                passed(dve, read, tile, back=back, per=BR, step=j + 2)
                for i, c in enumerate(HALVES if j == 0 else [slice(0, EC)]):
                    passed(dve, e_sb, tile, per=2, step=i + j + 1)
                    V.tensor_tensor(hm[0][:, j, c, :], ge[:, c, :], mexp[tile.s][:, j, c, :],
                                    ALU.mult).then_inc(done, 1)

            def part_lo(tile, gh_sb, gl_v, read, back):
                passed(dve, gh_sb, tile)
                passed(dve, read, tile, back=back, per=3)
                V.tensor_tensor(gl[:, :, :], ge[:, :, :], gh[:, :, :].bitcast(fp32), ALU.subtract).then_inc(gl_v, 1)

            def output(o):
                passed(dve, rl2_ps, o)
                link(V.tensor_tensor(yt[:, :], refined, pv("iw"), ALU.mult))
                passed(dve, base_g, o)
                if not isinstance(o.b, int) or o.b > 0:
                    dve.wait_ge(y_out[o.s], 16 * o.b)
                V.tensor_tensor(y[o.s][:, :], yt[:, :], base[o.s][:, :], ALU.add).then_inc(y_v, 1)

            def slot(t, k=None):
                z, f, n, m, o = t.at(2), t.at(1), t.at(-1), t.at(-2), t.at(-3)
                if k is None:
                    origin[0] = None
                else:
                    if not loop_start:
                        loop_start.append(links[0])
                    origin[0] = k * DVE_LINKS + loop_start[0]
                    links[1] = links[0]
                before = links[0]

                if m.exists() and not n.exists():
                    magnitude(m, u2_sb, abs2_v)
                if t.exists():
                    last_ps, last_g, back = (u2_ps, hl2_g, 2) if m.exists() else (u1_ps, hl1_g, 1)
                    mask_hi(t, 0, e1_sb, hm1_v, last_ps, back)
                    part_lo(t, gh1_sb, gl1_v, last_g, back)
                    mask_hi(t, 1, e1_sb, hm1_v, last_ps, back)
                if n.exists():
                    passed(dve, pq1_v, n)
                    link(V.tensor_scalar(acc[:, :, :], pq[:, 0, :, :], w3[n.s][:, 0:1], None, ALU.mult))
                    for j in range(1, BR):
                        link(V.scalar_tensor_tensor(acc[:, :, :], pq[:, j, :, :], w3[n.s][:, j:j + 1], acc[:, :, :],
                                                    ALU.mult, ALU.add))
                    passed(dve, th1_sb, n)
                    link(V.tensor_scalar(nh[:, :], th1[:, n.s:n.s + 1], -0.5, -0.5, ALU.mult, ALU.add))
                    passed(dve, u0_g, n)
                    link(V.tensor_scalar(t1[:, :], u0[n.s][:, :], nh[:, :], None, ALU.mult))
                    V.tensor_tensor(v1[n.s][:, :], acc[:, 0, :], t1[:, :], ALU.mult)
                    link(V.tensor_tensor(t2[:, :], acc[:, 1, :], t1[:, :], ALU.mult))
                    V.scalar_tensor_tensor(x1[n.s][:, :], t2[:, :], 0.05, xf[n.s][:, :], ALU.mult,
                                           ALU.add).then_inc(x1_v, 1)
                if t.exists():
                    passed(dve, tw_sb, t)
                    V.tensor_scalar(w3[t.s][:, 1:2], tw[:, :], 0.5, 0.5, ALU.mult, ALU.add)
                    link(V.tensor_scalar(w3[t.s][:, 2:3], tw[:, :], -0.5, 0.5, ALU.mult, ALU.add))
                    link(V.tensor_scalar(w3[t.s][:, 1:3], w3[t.s][:, 1:3], omsw, None, ALU.mult))
                if f.exists():
                    passed(dve, ex_sb, f)
                    link(V.reciprocal(rinv[:, :], esum[:, f.s:f.s + 1]))
                    passed(dve, att_ps, f)
                    passed(dve, hx_g, f, back=1)
                    link(V.tensor_scalar(h[:, :], pd[:, 0:D], rinv[:, :], None, ALU.mult))
                    link(V.bn_stats(st[:, :], h[:, :]))
                    passed(dve, rs1_g, f, back=1)
                    bearer()
                    V.bn_aggr(mv1[:, :], st[:, :]).then_inc(mv1_v, 1)
                if m.exists() and n.exists():
                    magnitude(m, u2_sb, abs2_v)
                if f.exists():
                    passed(dve, rs1_g, f)
                    passed(dve, mv1_v, f)
                    passed(dve, xnT_ps, f, back=1)
                    V.tensor_scalar(xn[:, :], h[:, :], mv1[:, 0:1], rs1[:, :], ALU.subtract,
                                    ALU.mult).then_inc(xn_v, 1)
                if m.exists():
                    for j in range(BR):
                        last = V.tensor_scalar(gw[:, j, :], tan[m.s][:, 1, j, :], 1.0, w3[m.s][:, j:j + 1],
                                               ALU.add, ALU.mult)
                    link(last)
                if t.exists():
                    magnitude(t, u1_sb, abs1_v)
                if o.exists() and n.exists():
                    output(o)
                if z.exists():
                    passed(dve, score_ps, z)
                    passed(dve, ex_sb, z, back=1)
                    link(V.tensor_scalar(sc[:, :], pd[:, 0:P], float(D) ** -0.5, None, ALU.mult, ALU.max,
                                         accum_out=smx[:, z.s:z.s + 1]))
                    V.tensor_scalar(nmx[:, z.s:z.s + 1], smx[:, z.s:z.s + 1], -1.0, None,
                                    ALU.mult).then_inc(smax_v, 1)
                    if z.low == 0:
                        split_biases()
                if n.exists():
                    shared_lo(n, s2_sb, sh2, sa2, sl2_v)
                if f.exists():
                    passed(dve, xnT_ps, f)
                    for q in range(KD):
                        carry = 0.0 if f.s == 0 else holo[f.s - 1][:, q, P - 1:P]
                        if f.s and q == 0:
                            passed(dve, scan_v, f, back=1)
                        last = V.tensor_tensor_scan(holo[f.s][:, q, :], decays[:, :], pc[:, q * P:(q + 1) * P], carry,
                                                    ALU.mult, ALU.add)
                    last.then_inc(scan_v, 1)
                if m.exists():
                    link(V.scalar_tensor_tensor(ga[:, :, :], tan[m.s][:, 2, :, :], 1.0, gw[:, :, :], ALU.add, ALU.mult))
                    link(V.tensor_tensor(t1[:, :], ga[:, 0, :], ga[:, 1, :], ALU.add))
                if n.exists():
                    if t.exists():
                        mask_hi(n, 0, e2_sb, hm2_v, u1_ps, -1)
                        part_lo(n, gh2_sb, gl2_v, hl1_g, -1)
                        mask_hi(n, 1, e2_sb, hm2_v, u1_ps, -1)
                    else:
                        mask_hi(n, 0, e2_sb, hm2_v, u2_ps, 1)
                        part_lo(n, gh2_sb, gl2_v, hl2_g, 1)
                        mask_hi(n, 1, e2_sb, hm2_v, u2_ps, 1)
                if f.exists():
                    passed(dve, retr_ps, f)
                    passed(dve, hx_g, f)
                    passed(dve, base_g, f, back=1)
                    link(V.tensor_tensor(h2[:, :], pd[:, 0:D], hx[:, :], ALU.add))
                    link(V.bn_stats(st[:, :], h2[:, :]))
                    bearer()
                    V.bn_aggr(mv2[:, :], st[:, :]).then_inc(mv2_v, 1)
                if m.exists():
                    link(V.tensor_tensor(t1[:, :], t1[:, :], ga[:, 2, :], ALU.add))
                    link(V.scalar_tensor_tensor(t1[:, :], t1[:, :], 0.5, v1[m.s][:, :], ALU.mult, ALU.mult))
                if f.exists():
                    passed(dve, rs2_g, f)
                    passed(dve, mv2_v, f)
                    V.tensor_scalar(xf[f.s][:, :], h2[:, :], mv2[:, 0:1], rs2[:, :], ALU.subtract,
                                    ALU.mult).then_inc(xf_v, 1)
                    if f.low == 0:
                        split_shared()
                if m.exists():
                    passed(dve, ln2_sb, m)
                    link(V.tensor_tensor(sp2[:, :, :], rb[m.s][:, :, :], tan[m.s][:, 0, :, :], ALU.subtract))
                    link(V.tensor_tensor(sp2[:, :, :], sp2[:, :, :], gw[:, :, :], ALU.mult))
                    passed(dve, th2_sb, m)
                    V.tensor_scalar(h2c[:, :], th2[:, m.s:m.s + 1], 0.025, 0.025, ALU.mult, ALU.add)
                    link(V.tensor_tensor(t2[:, :], sp2[:, 0, :], sp2[:, 1, :], ALU.add))
                    link(V.tensor_tensor(t2[:, :], t2[:, :], sp2[:, 2, :], ALU.add))
                    passed(dve, u1_g, m)
                    link(V.tensor_tensor(t2[:, :], t2[:, :], u1[:, :], ALU.mult))
                    link(V.tensor_tensor(t1[:, :], t1[:, :], t2[:, :], ALU.subtract))
                    passed(dve, x2T_ps, m, back=1)
                    V.scalar_tensor_tensor(x2[:, :], t1[:, :], h2c[:, :], x1[m.s][:, :], ALU.mult,
                                           ALU.add).then_inc(x2_v, 1)
                if o.exists() and not n.exists():
                    output(o)
                if f.exists():
                    passed(dve, lg_ps, f)
                    link(V.tensor_tensor(lg[:, :], pd[:, 0:E], pv("b2r"), ALU.add))
                    bearer()
                    link(V.max(top[:, :], lg[:, :]))
                    passed(dve, tw_sb, f, back=1)
                    V.tensor_tensor(dif[:, :], top[:, 0:1], top[:, 1:2], ALU.subtract).then_inc(dif_v, 1)
                    link(V.max_index(topi[:, :], top[:, :], lg[:, :]))
                    link(V.tensor_copy(topf[:, :], topi[:, 0:2]))
                    passed(dve, mT_ps, f, back=1)
                    for j in range(2):
                        last = V.tensor_scalar(mask[:, j, :], pv("iota"), topf[:, j:j + 1], None, ALU.is_equal)
                    last.then_inc(mask_v, 1)
                    shared_lo(f, s1_sb, sh1, sa1, sl1_v)
                if t.exists():
                    passed(dve, ln1_sb, t)
                    sp = pq[:, :, 0, :]
                    link(V.tensor_tensor(sp, rb[t.s][:, :, :], tan[t.s][:, 0, :, :], ALU.subtract))
                    V.scalar_tensor_tensor(pq[:, :, 1, :], tan[t.s][:, 1, :, :], 1.0, sp, ALU.add,
                                           ALU.mult).then_inc(pq1_v, 1)
                if k is not None:
                    assert links[0] - before == DVE_LINKS, links[0] - before

            loop_start = []

            def slots(t, k=None):
                if k is None and loop_start and links[0] < loop_start[0] + DVE_LINKS * full_slots:
                    links[0] = loop_start[0] + DVE_LINKS * full_slots
                slot(t, k)

            full_slots = NS * TURNS
            run(dve, slots)


def _pack(i):
    import numpy as np
    a = {n: np.zeros((P, w), np.float32) for n, w in _ALL}
    a["ident"][:] = np.eye(P)
    for c in range(EC):
        for e in range(P // HID):
            a["expand"][c * (P // HID) + e, c * P + e * HID:c * P + (e + 1) * HID] = 1
    a["iota"][:] = np.tile(np.arange(E), 3)
    a["part"][E:3 * E, 0] = -1
    a["part"][2 * E:3 * E, 1] = -1
    a["part"][HID, 2] = 1
    a["part"][:, 3] = 1 - a["part"][:, 2]
    turn = (-(np.arange(D)[:, None] + np.arange(D)[None, :])) % D
    for name, key in (("bind", "L0_attn_bind_key"), ("unbind", "L0_attn_unbind_key")):
        a[name][:] = i[key][turn].reshape(KD, P, D).transpose(1, 0, 2).reshape(P, KD * D)
    a["decay"][:] = i["L0_attn_decay"]
    a["gate"][:] = i["L0_attn_gate"]
    f = {k[len("L0_ffn_"):]: v for k, v in i.items() if k.startswith("L0_ffn_")}
    a["sw"][:] = f["shared_weight"]
    chunks = lambda w: w.reshape(-1, P, w.shape[1]).transpose(1, 0, 2)
    a["w1r"][:] = chunks(f["router_w1"]).reshape(P, -1)
    a["b1r"][0:HID, 0] = f["router_b1"]
    a["w2r"][0:HID] = f["router_w2"]
    a["b2r"][:] = f["router_b2"]
    a["mu"][:] = f["mu"]
    a["iw"][:] = f["integration_weight"]
    a["rb2"][:] = f["refine_b2"]
    w1 = f["expert_w1"].transpose(1, 0, 2).reshape(2 * D, E * HID)
    a["w1e"][:] = chunks(w1).reshape(P, -1)
    s = a["w1s"].reshape(P, 2 * KD, P)
    s[:, :, 0:HID] = chunks(f["shared_w1"])
    s[:, 0:KD, HID:P] = chunks(f["halt_w1"])
    order = np.r_[D:3 * D, 0:D]
    a["w2e"][:] = chunks(f["expert_w2"].reshape(E * HID, 3 * D)[:, order]).reshape(P, -1)
    a["w2sa"][:] = np.tile(f["shared_w2"][:, order], (P // HID, 1))
    a["w2sb"][0:HID] = f["shared_w2"][:, order]
    a["w2sb"][HID:HID + 2] = f["shared_b2"][order]
    a["w2h"][HID:P] = f["halt_w2"]
    a["r1"][:] = chunks(f["refine_w1"]).reshape(P, -1)
    a["r2"][:] = chunks(f["refine_w2"]).reshape(P, -1)
    for r in range(3):
        a["b2"][r * E:(r + 1) * E] = f["expert_b2"][:, order]
    a["b1e"][:] = f["expert_b1"].reshape(EC, P).T
    a["b1s"][:, 0] = np.r_[f["shared_b1"], f["halt_b1"]]
    a["rb1"][:] = f["refine_b1"].reshape(REF // P, P).T
    a["hb2"][:] = f["halt_b2"]
    return np.concatenate([a[n] for n, _ in _ALL], axis=1)


def kernel(**inputs):
    import numpy as _np
    import concourse.bacc as _bacc
    from concourse import mybir as _mybir
    from concourse.bass_utils import run_bass_kernel_spmd as _run

    i = {k: _np.asarray(v) for k, v in inputs.items()}
    arrays = {"x_dram": _np.ascontiguousarray(i["x"].reshape(BATCH * SEQ, D)), "params_dram": _pack(i)}
    nc = _bacc.Bacc("TRN2", target_bir_lowering=False, num_devices=1)
    args = [nc.dram_tensor(n, a.shape, _mybir.dt.from_np(a.dtype), kind="ExternalInput").ap()
            for n, a in arrays.items()]
    out = nc.dram_tensor("out_dram", (NT * P, D), _mybir.dt.float32, kind="ExternalOutput").ap()
    audio_layer(nc, *args, out)
    r = _run(nc, [arrays], core_ids=[0])
    return r.results[0]["out_dram"].reshape(BATCH, NS * P, D)
```
